# Optimizing a Trainium2 kernel written in Bass

```python
import numpy as np
import jax
import jax.numpy as jnp

def _softmax(x, axis=-1):
    return jax.nn.softmax(x, axis=axis)

def _gelu(x):
    return jax.nn.gelu(x, approximate=True)

def _silu(x):
    return jax.nn.silu(x)

def _sigmoid(x):
    return jax.nn.sigmoid(x)

def _layernorm(x, axis=-1, eps=1e-05):
    m = jnp.mean(x, axis=axis, keepdims=True)
    v = jnp.var(x, axis=axis, keepdims=True)
    return (x - m) / jnp.sqrt(v + eps)

def _scatter_add(tgt, idx, src, axis=0):
    return tgt.at[idx].add(src)

def _segment_sum(src, seg, n):
    return jax.ops.segment_sum(src, seg, n)
kernel_name = 'mk_conv_preact_d4_conv_nchw16_r2_52a106'

def setup_inputs(seed: int=0):
    np.random.seed(seed)
    _w = jnp.asarray

    def _rec_inputs():
        import jax
        import jax.numpy as jnp
        _gk = jax.random.key(seed)
        x = -0.0005207 + 1.001 * jax.random.normal(jax.random.fold_in(_gk, 1), (8, 16, 64, 64), jnp.float32)
        return x
    x = _rec_inputs()

    def _L0_conv_setup():
        import jax, jax.numpy as jnp
        import numpy as np
        from jax import lax
        NUM_COLS = 4
        NUM_ROWS = 4
        C = 16
        K = 3
        B, H, Wd = (8, 64, 64)
        W_SCALE = 0.05

        def _cell(w, bias, ins):
            if len(ins) < 3:
                pad_shape = (ins[0].shape[0], (3 - len(ins)) * C) + ins[0].shape[2:]
                ins = ins + [jnp.zeros(pad_shape, dtype=ins[0].dtype)]
            x = jnp.concatenate(ins, axis=1)
            y = lax.conv_general_dilated(x, w, window_strides=(1, 1), padding='SAME', dimension_numbers=('NCHW', 'OIHW', 'NCHW'))
            y = jax.nn.relu(y + bias[None, :, None, None])
            right, up, down = jnp.split(y, 3, axis=1)
            return (right, up, down)
        key = jax.random.key(seed)
        k1, k2 = jax.random.split(key, 2)
        x = jax.random.normal(k1, (B, C, H, Wd), dtype=jnp.float32)
        W = jax.random.normal(k2, (NUM_COLS, NUM_ROWS, 3 * C, 3 * C, K, K), dtype=jnp.float32) * W_SCALE
        b = jnp.zeros((NUM_COLS, NUM_ROWS, 3 * C), dtype=jnp.float32)
        return {'input_tensor': x, 'W': W, 'b': b}
    _L0_conv_all = _L0_conv_setup()
    _L0_conv_in = {k: v for k, v in _L0_conv_all.items() if k in ('W', 'b')}
    del _L0_conv_all

    def _L1_conv_setup():
        import jax, jax.numpy as jnp
        import numpy as np
        K_SIZE = 3
        PAD = K_SIZE // 2

        def _diag_L(n, k):
            half = k // 2
            d = np.zeros(n, dtype=np.float32)
            d[:half] = 1.0
            d[n - half:] = 1.0
            if 2 * half < k:
                d[half] = 1.0
            return d

        def _circular_pad(w, H, W, k, p):
            w = jnp.roll(jnp.pad(jnp.flip(w, -1), ((0, 0), (0, 0), (0, 0), (0, W - k))), -p, axis=-1)
            w = jnp.roll(jnp.pad(jnp.flip(w, -2), ((0, 0), (0, 0), (0, H - k), (0, 0))), -p, axis=-2)
            return w
        key = jax.random.key(seed)
        kx, kw = jax.random.split(key)
        x = jax.random.normal(kx, (16, 16, 128, 128), dtype=jnp.float32)
        weight = jax.random.normal(kw, (16, 16, 3, 3), dtype=jnp.float32) * (2.0 / (16 * 9)) ** 0.5
        return {'x': x, 'weight': weight}
    _L1_conv_all = _L1_conv_setup()
    _L1_conv_in = {k: v for k, v in _L1_conv_all.items() if k in ('weight',)}
    del _L1_conv_all

    def _L2_conv_setup():
        import jax, jax.numpy as jnp
        import numpy as np
        GRID_SIZE = 5
        SPLINE_ORDER = 3
        KSIZE = 3
        STRIDE = 1
        PAD = 1
        NBASES = GRID_SIZE + SPLINE_ORDER

        def _grid():
            h = 2.0 / GRID_SIZE
            return jnp.arange(-SPLINE_ORDER, GRID_SIZE + SPLINE_ORDER + 1, dtype=jnp.float32) * h - 1.0

        def _b_splines(x, grid):
            x = x[..., None]
            bases = ((x >= grid[:-1]) & (x < grid[1:])).astype(x.dtype)
            for k in range(1, SPLINE_ORDER + 1):
                left = (x - grid[:-(k + 1)]) / (grid[k:-1] - grid[:-(k + 1)]) * bases[..., :-1]
                right = (grid[k + 1:] - x) / (grid[k + 1:] - grid[1:-k]) * bases[..., 1:]
                bases = left + right
            return bases

        def _extract_patches(x, k, stride, padding):
            if padding > 0:
                x = jnp.pad(x, ((0, 0), (0, 0), (padding, padding), (padding, padding)))
            B, C, H, W = x.shape
            oh = (H - k) // stride + 1
            ow = (W - k) // stride + 1
            cols = [x[:, :, dh:dh + (oh - 1) * stride + 1:stride, dw:dw + (ow - 1) * stride + 1:stride] for dh in range(k) for dw in range(k)]
            return jnp.stack(cols, axis=-1)
        key = jax.random.key(seed)
        ks = jax.random.split(key, 5)
        B, Cin, Cout, H, W = (4, 16, 16, 64, 64)
        k2 = KSIZE * KSIZE
        x = jax.random.normal(ks[0], (B, Cin, H, W), dtype=jnp.float32)
        base_weight = jax.random.normal(ks[1], (Cout, Cin, k2, k2), dtype=jnp.float32) * (1.0 / np.sqrt(k2))
        spline_weight = jax.random.normal(ks[2], (Cout, Cin, k2, k2, NBASES), dtype=jnp.float32) * 0.1
        spline_scaler = jax.random.normal(ks[3], (Cout, Cin, k2, k2), dtype=jnp.float32) * (1.0 / np.sqrt(k2))
        bias_weight = jax.random.normal(ks[4], (Cout,), dtype=jnp.float32)
        return {'x': x, 'base_weight': base_weight, 'spline_weight': spline_weight, 'spline_scaler': spline_scaler, 'bias_weight': bias_weight}
    _L2_conv_all = _L2_conv_setup()
    _L2_conv_in = {k: v for k, v in _L2_conv_all.items() if k in ('base_weight', 'spline_weight', 'spline_scaler', 'bias_weight')}
    del _L2_conv_all

    def _L3_conv_setup():
        import jax, jax.numpy as jnp
        import numpy as np
        key = jax.random.key(seed)
        k1, k2, k3 = jax.random.split(key, 3)
        B, C, O, NF = (4, 16, 16, 9)
        x = jax.random.normal(k1, (B, C, 225, 240), dtype=jnp.float32)
        combinator = jax.random.normal(k2, (O, C * NF), dtype=jnp.float32) * 0.05
        bias = jax.random.normal(k3, (O,), dtype=jnp.float32) * 0.05
        return {'x': x, 'combinator': combinator, 'bias': bias}
    _L3_conv_all = _L3_conv_setup()
    _L3_conv_in = {k: v for k, v in _L3_conv_all.items() if k in ('combinator', 'bias')}
    del _L3_conv_all
    return {'x': x, 'L0_conv_W': _L0_conv_in['W'], 'L0_conv_b': _L0_conv_in['b'], 'L1_conv_weight': _L1_conv_in['weight'], 'L2_conv_base_weight': _L2_conv_in['base_weight'], 'L2_conv_spline_weight': _L2_conv_in['spline_weight'], 'L2_conv_spline_scaler': _L2_conv_in['spline_scaler'], 'L2_conv_bias_weight': _L2_conv_in['bias_weight'], 'L3_conv_combinator': _L3_conv_in['combinator'], 'L3_conv_bias': _L3_conv_in['bias']}

def reference(x, L0_conv_W, L0_conv_b, L1_conv_weight, L2_conv_base_weight, L2_conv_spline_weight, L2_conv_spline_scaler, L2_conv_bias_weight, L3_conv_combinator, L3_conv_bias):
    import jax
    import jax.numpy as jnp

    def _L0_conv_ref(input_tensor, W, b):
        import jax, jax.numpy as jnp
        import numpy as np
        from jax import lax
        NUM_COLS = 4
        NUM_ROWS = 4
        C = 16
        K = 3
        B, H, Wd = (8, 64, 64)
        W_SCALE = 0.05

        def _cell(w, bias, ins):
            if len(ins) < 3:
                pad_shape = (ins[0].shape[0], (3 - len(ins)) * C) + ins[0].shape[2:]
                ins = ins + [jnp.zeros(pad_shape, dtype=ins[0].dtype)]
            x = jnp.concatenate(ins, axis=1)
            y = lax.conv_general_dilated(x, w, window_strides=(1, 1), padding='SAME', dimension_numbers=('NCHW', 'OIHW', 'NCHW'))
            y = jax.nn.relu(y + bias[None, :, None, None])
            right, up, down = jnp.split(y, 3, axis=1)
            return (right, up, down)
        outs = [None] * NUM_ROWS
        for col in range(NUM_COLS):
            for row in range(NUM_ROWS):
                if col == 0:
                    ins = [input_tensor] if row == 0 else [outs[row - 1][-1]]
                elif row == 0:
                    ins = [outs[row][0], outs[row + 1][1]]
                elif row == NUM_ROWS - 1:
                    ins = [outs[row][0], outs[row - 1][-1]]
                else:
                    ins = [outs[row][0], outs[row + 1][1], outs[row - 1][-1]]
                outs[row] = _cell(W[col, row], b[col, row], ins)
        return outs[-1][0]

    def _L1_conv_ref(x, weight):
        import jax, jax.numpy as jnp
        import numpy as np
        K_SIZE = 3
        PAD = K_SIZE // 2

        def _diag_L(n, k):
            half = k // 2
            d = np.zeros(n, dtype=np.float32)
            d[:half] = 1.0
            d[n - half:] = 1.0
            if 2 * half < k:
                d[half] = 1.0
            return d

        def _circular_pad(w, H, W, k, p):
            w = jnp.roll(jnp.pad(jnp.flip(w, -1), ((0, 0), (0, 0), (0, 0), (0, W - k))), -p, axis=-1)
            w = jnp.roll(jnp.pad(jnp.flip(w, -2), ((0, 0), (0, 0), (0, H - k), (0, 0))), -p, axis=-2)
            return w
        B, Ci, H, W = x.shape
        k, p = (K_SIZE, PAD)
        w_pad = _circular_pad(weight, H, W, k, p)
        dL = jnp.asarray(np.outer(_diag_L(H, k), _diag_L(W, k)))
        Lw = jnp.fft.fft2(w_pad * dL)
        Kx = jnp.fft.ifft2(x, norm='ortho')
        z = jnp.einsum('oihw,bihw->bohw', Lw, Kx)
        y = jnp.fft.fft2(z, norm='ortho')
        return jnp.real(y).astype(x.dtype)

    def _L2_conv_ref(x, base_weight, spline_weight, spline_scaler, bias_weight):
        import jax, jax.numpy as jnp
        import numpy as np
        GRID_SIZE = 5
        SPLINE_ORDER = 3
        KSIZE = 3
        STRIDE = 1
        PAD = 1
        NBASES = GRID_SIZE + SPLINE_ORDER

        def _grid():
            h = 2.0 / GRID_SIZE
            return jnp.arange(-SPLINE_ORDER, GRID_SIZE + SPLINE_ORDER + 1, dtype=jnp.float32) * h - 1.0

        def _b_splines(x, grid):
            x = x[..., None]
            bases = ((x >= grid[:-1]) & (x < grid[1:])).astype(x.dtype)
            for k in range(1, SPLINE_ORDER + 1):
                left = (x - grid[:-(k + 1)]) / (grid[k:-1] - grid[:-(k + 1)]) * bases[..., :-1]
                right = (grid[k + 1:] - x) / (grid[k + 1:] - grid[1:-k]) * bases[..., 1:]
                bases = left + right
            return bases

        def _extract_patches(x, k, stride, padding):
            if padding > 0:
                x = jnp.pad(x, ((0, 0), (0, 0), (padding, padding), (padding, padding)))
            B, C, H, W = x.shape
            oh = (H - k) // stride + 1
            ow = (W - k) // stride + 1
            cols = [x[:, :, dh:dh + (oh - 1) * stride + 1:stride, dw:dw + (ow - 1) * stride + 1:stride] for dh in range(k) for dw in range(k)]
            return jnp.stack(cols, axis=-1)
        patches = _extract_patches(x, KSIZE, STRIDE, PAD)
        grid = _grid()
        bspl = _b_splines(patches, grid)
        base_w = base_weight.sum(axis=2)
        spl_w = (spline_weight * spline_scaler[..., None]).sum(axis=2)
        out = jnp.einsum('bjhwn,ijn->bihw', jax.nn.silu(patches), base_w)
        out = out + jnp.einsum('bjhwns,ijns->bihw', bspl, spl_w)
        out = out + bias_weight[None, :, None, None]
        return out

    def _L3_conv_ref(x, combinator, bias):
        import jax, jax.numpy as jnp
        import numpy as np
        O = combinator.shape[0]
        C = x.shape[1]
        w = combinator.reshape(O, 3, 3, C).transpose(0, 3, 1, 2)
        out = jax.lax.conv_general_dilated(x, w, window_strides=(1, 1), padding=((1, 1), (1, 1)), dimension_numbers=('NCHW', 'OIHW', 'NCHW'))
        return out + bias[None, :, None, None]

    def _gn(v, G=8, eps=1e-05):
        B_, C_, H_, W_ = v.shape
        g = v.reshape(B_, G, C_ // G, H_, W_)
        m = jnp.mean(g, axis=(2, 3, 4), keepdims=True)
        s = jnp.var(g, axis=(2, 3, 4), keepdims=True)
        return ((g - m) / jnp.sqrt(s + eps)).reshape(v.shape)

    def _ln_c(v, eps=1e-06):
        m = jnp.mean(v, axis=1, keepdims=True)
        s = jnp.var(v, axis=1, keepdims=True)
        return (v - m) / jnp.sqrt(s + eps)

    def _ln_t(v, eps=1e-05):
        m = jnp.mean(v, axis=-1, keepdims=True)
        s = jnp.var(v, axis=-1, keepdims=True)
        return (v - m) / jnp.sqrt(s + eps)

    def _to_tokens(v):
        B_, C_, H_, W_ = v.shape
        return v.reshape(B_, C_, H_ * W_).transpose(0, 2, 1)

    def _from_tokens(t, like):
        B_, C_, H_, W_ = like.shape
        return t.transpose(0, 2, 1).reshape(B_, C_, H_, W_)
    x = x + _L0_conv_ref(_gn(x), L0_conv_W, L0_conv_b)
    x = x + _L1_conv_ref(_gn(x), L1_conv_weight)
    x = x + _L2_conv_ref(_gn(x), L2_conv_base_weight, L2_conv_spline_weight, L2_conv_spline_scaler, L2_conv_bias_weight)
    x = x + _L3_conv_ref(_gn(x), L3_conv_combinator, L3_conv_bias)
    return x

_drawn_inputs = setup_inputs


def setup_inputs(seed=0):
    import zlib

    import numpy as np

    out = dict(_drawn_inputs(seed))
    spreads = {'L0_conv_b': (0.0, 0.275)}
    factors = {'L3_conv_bias': 8.0}
    for name, (base, spread) in spreads.items():
        noise = np.random.default_rng([zlib.crc32(name.encode()), seed]).standard_normal(out[name].shape)
        drawn = base * np.exp(spread * noise) if base else spread * noise
        out[name] = jnp.asarray(drawn.astype(out[name].dtype))
    for name, factor in factors.items():
        out[name] = (out[name] * factor).astype(out[name].dtype)
    return out
```

```python
from contextlib import ExitStack

import numpy as np
import concourse.bass as bass
from concourse import mybir

P = 128
C = 16
YI = 8
YB = 8
WD = 64
PW = WD + 2
PIX = YB * WD
B = 8
HALVES = 2
NB = B // HALVES
HALO = 2 * C
K3 = 3
NG = 3
TAP_SLOTS = 9
LEAD = 6
WIN = LEAD + TAP_SLOTS * 9
MAIN_TILES = 27
TILES = 36
FSLOTS = 8
BASES = 8
FEATS = BASES + 1

RIGHT, UP, DOWN = range(3)
GN_EPS = 1e-5


class Count:

    def __init__(self):
        self.base, self.n = 0, 0

    def next(self):
        self.n += 1
        return self.base + self.n

    def enter(self, base):
        self.base, self.n = base, 0


def lattice():
    cells = []
    for col in range(4):
        for row in range(4):
            if col == 0:
                ins = [0] if row == 0 else [3 + row]
            elif row == 0:
                ins = [0, 4]
            elif row == 3:
                ins = [3, 6]
            else:
                ins = [row, 4 + row, 3 + row]
            outs = []
            if col < 3 or row == 3:
                outs.append((RIGHT, row))
            if row > 0 and col < 3:
                outs.append((UP, 3 + row))
            if row < 3:
                outs.append((DOWN, 4 + row))
            cells.append((col * 4 + row, ins, outs))
    return cells


def build(nc, x, l0w, l0b, l1w, l2base, l2spline, l2scale, l2bias, l3w, l3bias, consts, out):
    F32, F32R = mybir.dt.float32, mybir.dt.float32r
    ALU, ACT = mybir.AluOpType, mybir.ActivationFunctionType
    cells = lattice()
    NC = len(cells)

    tiles_before, outs_before, chunks_before, halo_before = [0], [0], [0], [0]
    for _, ins, outs in cells:
        tiles_before.append(tiles_before[-1] + NB * (len(ins) + 1))
        outs_before.append(outs_before[-1] + NB * len(outs))
        chunks_before.append(chunks_before[-1] + K3 * (len(ins) + 1))
        halo_before.append(halo_before[-1] + NB // 2 * 2 * len(ins) * 16)
    TH, OH, CH, HH = tiles_before[-1], outs_before[-1], chunks_before[-1], halo_before[-1]
    assert CH % 2 == 0
    T_AT = [HALVES * TH, HALVES * TH + 2 * B, HALVES * TH + 2 * B + 12 * B]
    O_AT = {1: HALVES * OH, 3: HALVES * OH + B}
    C_AT = [HALVES * CH, HALVES * CH + 6, HALVES * CH + 42]
    H_AT = [HALVES * HH, HALVES * HH + B // 2 * 4 * 16, HALVES * HH + B // 2 * 4 * 16 + B // 2 * 6 * 16]
    FILL_AT = [HALVES * NC, HALVES * NC + 1, HALVES * NC + 4]

    ctx = ExitStack()
    with ctx:
        def sb(name, shape, dt=F32):
            return ctx.enter_context(nc.sbuf_tensor(name, shape, dt))

        def sem(name):
            return ctx.enter_context(nc.semaphore(name))

        X = sb("X", [P, B, PIX])
        S = sb("S", [P, 7, NB, PIX])
        F = sb("F", [P, FSLOTS, 2, YB, PW], F32R)
        W = sb("W", [P, 2, 2, TILES, P], F32R)
        HS = sb("HS", [3 * HALO, 2, YB, PW])
        WIN_T = sb("WIN_T", [NG * C, 2, WIN, C], F32R)
        WH = sb("WH", [NG * C, 2, K3, 2 * NG, C], F32R)
        RAW = sb("RAW", [NG * C, NG * C * 9])
        KAN = sb("KAN", [C, FEATS, C, 9])
        G = sb("G", [P, P])
        CB = sb("CB", [P, 16])
        IDF = sb("IDF", [NG * C, NG * C])
        ID = sb("ID", [NG * C, NG * C], F32R)
        BN_IN = sb("BN_IN", [NG * C, C])
        BN_REP = sb("BN_REP", [NG * C, YI, C])
        BIAS = sb("BIAS", [P, NG * C])
        OB_IN = sb("OB_IN", [2, C])
        OB_REP = sb("OB_REP", [2, YI, C])
        OB = sb("OB", [P, 2])
        STATS = sb("STATS", [P, B, 6])
        MV = sb("MV", [P, B, 2])
        GM = sb("GM", [P, B, 2])
        NV = sb("NV", [P, B])
        VE = sb("VE", [P, B])
        MASK = CB[:, BASES + 3:BASES + 5]
        NHALF = sb("NHALF", [P, B])
        RS = sb("RS", [P, B])
        NBI = sb("NBI", [P, B])

        flat = S[:, :, :, :].rearrange("p a b n -> p (a b n)")
        TS = YB * PW

        def carve(k):
            return flat[:, k * TS:(k + 1) * TS].rearrange("p (y w) -> p y w", w=PW)

        NS1 = [carve(0), carve(1)]
        H1 = [carve(2), carve(3)]
        NS = [carve(4), carve(5)]
        UA = [carve(6 + i) for i in range(3)]
        TA = [carve(9 + i) for i in range(3)]
        TB = [carve(12 + i) for i in range(3)]
        A2 = [carve(15 + i) for i in range(2)]
        B2 = [carve(17 + i) for i in range(3)]
        FT = [carve(20 + i) for i in range(3)]
        assert 23 * TS <= 7 * NB * PIX

        PB = [ctx.enter_context(nc.psum_tensor(f"PB{i}", [P, 512], F32)) for i in range(8)]
        OUT_BANK = PB[0:3]
        BUILD_HI, BUILD_LO = PB[3:5], PB[5:7]
        STAT_BANK = [PB[7], PB[2]]

        x_loaded = sem("x_loaded")
        const_loaded = sem("const_loaded")
        taps_loaded = sem("taps_loaded")
        kan_loaded = sem("kan_loaded")
        kan_chunk = sem("kan_chunk")
        pool_step = sem("pool_step")
        halo_loaded = [sem("halo_loaded0"), sem("halo_loaded1")]
        win_clear = sem("win_clear")
        w_clear = sem("w_clear")
        hs_clear = sem("hs_clear")
        f_clear = sem("f_clear")
        id_ready = sem("id_ready")
        pool_const = sem("pool_const")
        bias_rep = sem("bias_rep")
        bias_done = sem("bias_done")
        bias_ready = sem("bias_ready")
        mv_ready = sem("mv_ready")
        group_ready = sem("group_ready")
        nv_ready = sem("nv_ready")
        norm_ready = sem("norm_ready")
        xn_ready = sem("xn_ready")
        dve_step = sem("dve_step")
        act_step = sem("act_step")
        hi_ready = sem("hi_ready")
        lo_ready = sem("lo_ready")
        out_done = sem("out_done")
        evac_done = sem("evac_done")
        tile_used = sem("tile_used")
        added = sem("added")
        pool_norm = sem("pool_norm")
        win_hi = sem("win_hi")
        win_lo = sem("win_lo")
        chunk_hi = sem("chunk_hi")
        chunk_lo = sem("chunk_lo")
        w_hi = sem("w_hi")
        w_lo = sem("w_lo")
        basis_u = sem("basis_u")
        basis_a = sem("basis_a")
        basis_b = sem("basis_b")
        basis_b3 = sem("basis_b3")
        feat_ready = sem("feat_ready")
        passed = {name: sem("passed_" + name) for name in ("sp", "dve", "pool")}
        scratch_clear = sem("scratch_clear")
        out_staged = sem("out_staged")
        stored = sem("stored")

        block = ctx.enter_context(nc.Block())
        XV = X[:, :, :].rearrange("p b (y x) -> p b y x", x=WD)
        SV = S[:, :, :, :].rearrange("p s b (y x) -> p s b y x", x=WD)

        def ximg(b):
            return X[:, bass.ds(b, 1), :].rearrange("p a (y x) -> p (a y) x", x=WD)

        def ximg_flat(b):
            return X[:, bass.ds(b, 1), :].rearrange("p a n -> p (a n)")

        def weight_dest(part, parity, kind, base, n_out, q):
            tiles = W[0:(P if kind == "main" else 3 * HALO), parity, part, base + q * n_out:base + (q + 1) * n_out, :]
            tiles = tiles.rearrange("p g (j c) -> p j g c", c=C)
            return tiles if kind == "main" else tiles[:, 0:YI:YI - 1]

        def out_bank(outs, o, b):
            return OUT_BANK[o] if len(outs) > 1 else OUT_BANK[b % 2]

        def flat2(a):
            return a.rearrange("p y w -> p (y w)")

        def pass_wait(eng, counter):
            eng.sem_inc(counter, 1)

        def at_half(h, per, n):
            return n if h is None else h * per + n

        ENTRIES = [(par, t) for par in range(2) for t in range(FEATS + 3)]
        ENTRIES_PER_PAIR = len(ENTRIES)
        BASES_PER_PAIR = 2 * (BASES + 3)
        PER = FEATS + 3

        def basis_parts(t):
            return P if t < BASES else (0, 3 * HALO, 3 * HALO, 2 * HALO)[t - BASES]

        LINKS_PER_IMAGE = 5
        PAIR_LINKS = 2 * (3 * (BASES + 3) + 2) + 2 * LINKS_PER_IMAGE
        TILES_OF = {1: 2, 2: PER, 3: 2}

        def fill_chunks(n_in, n_out, main_base, halo_base):
            return ([("main", q, main_base, n_out) for q in range(K3 * n_in)]
                    + [("halo", dx, halo_base, n_out) for dx in range(K3)])

        CELL_FILL = [fill_chunks(len(ins), NG, 0, MAIN_TILES) for _, ins, _ in cells]
        FILL1 = fill_chunks(1, 1, 0, MAIN_TILES)
        FILL2 = [fill_chunks(3, 1, 9 * t, MAIN_TILES + K3 * t) for t in range(3)]

        def source(bank, kind, n_out):
            if kind == "main":
                return bank[:, 0:YI * n_out * C].rearrange("p (j g c) -> p j g c", g=n_out, c=C)
            return bank[0:3 * HALO, 0:n_out * C].rearrange("p (g c) -> p g c", c=C)

        def raw_taps(kind, g0, n, dx):
            if kind == "cell":
                v = RAW[:, :].rearrange("o (g c k d) -> o g d k c", g=NG, c=C, k=K3)
            elif kind == "kan":
                v = KAN[:, :, :, :].rearrange("o g c (k d) -> o g d k c", k=K3)
            elif kind == "circular":
                v = RAW[0:C, 0:C * 9].rearrange("o (g c k d) -> o g d k c", g=1, c=C, k=K3)
            else:
                v = RAW[0:C, 0:C * 9].rearrange("o (g k d c) -> o g d k c", g=1, k=K3, c=C)
            return v[:, g0:g0 + n, dx]

        def fill_windows(eng, part, kind, g0, n, done):
            co = NG * C if kind == "cell" else C
            windows = [WIN_T[0:co, i, LEAD:WIN].rearrange("o (g d t) c -> o g d t c", g=NG, d=K3) for i in range(2)]
            edges = WH[0:co, part].rearrange("o d (g s) c -> o d g s c", g=NG)
            rows = [(ky, ky + 1) for ky in range(K3)] if kind == "circular" else [(0, K3)]
            for dx in range(K3):
                raw = raw_taps(kind, g0, n, K3 - 1 - dx if kind == "circular" else dx)
                for lo, up in rows:
                    src = raw[:, :, K3 - up:K3 - lo] if kind == "circular" else raw
                    dst = windows[part][:, 0:n, dx, lo:up]
                    if part == 0:
                        eng.activation(dst, src, ACT.Copy)
                    else:
                        eng.tensor_tensor(dst, src, windows[0][:, 0:n, dx, lo:up].bitcast(F32), ALU.subtract)
                for side in range(2):
                    ky = 2 * side
                    src = raw[:, :, K3 - 1 - ky if kind == "circular" else ky]
                    dst = edges[:, dx, 0:n, side]
                    if part == 0:
                        last = eng.activation(dst, src, ACT.Copy)
                    else:
                        last = eng.tensor_tensor(dst, src, windows[0][:, 0:n, dx, ky].bitcast(F32), ALU.subtract)
            last.then_inc(done, 1)

        @block.sync
        def _(sp):
            xv = x.rearrange("b c (yb yi) w -> b yi c yb w", yi=YI)
            for b in range(B):
                for yi in range(0, YI, 2):
                    sp.dma_start(XV[C * yi:C * (yi + 1), b], xv[b, yi]).then_inc(x_loaded, 16)
            sp.dma_start(G[:, :], consts[:, 0:P]).then_inc(const_loaded, 16)
            sp.dma_start(IDF[:, :], consts[0:NG * C, P:P + NG * C]).then_inc(const_loaded, 16)
            sp.dma_start(CB[:, :], consts[:, P + NG * C:P + NG * C + 16]).then_inc(const_loaded, 16)
            sp.dma_start(BN_IN[:, :], l0b.rearrange("a r (g c) -> (a r g) c", c=C)).then_inc(const_loaded, 16)
            sp.dma_start(OB_IN[0:1, :], l2bias.rearrange("(a c) -> a c", a=1)).then_inc(const_loaded, 16)
            sp.dma_start(OB_IN[1:2, :], l3bias.rearrange("(a c) -> a c", a=1)).then_inc(const_loaded, 16)

            def wait_both(sem_a, a, sem_b, b):
                sp.wait_ge(sem_a, a)
                pass_wait(sp, passed["sp"])
                sp.wait_ge(sem_b, b)
                pass_wait(sp, passed["sp"])

            def load_taps(k):
                sp.dma_start(RAW[:, :], l0w[k // 4, k % 4].rearrange("o i k d -> o (i k d)"))\
                  .then_inc(taps_loaded, 16)

            sp.wait_ge(hs_clear, 1)
            load_taps(0)
            with sp.Fori(0, HALVES) as h:
                wait_both(win_hi, h * NC + 1, win_lo, h * NC + 1)
                load_taps(1)
                for k, (_, ins, outs) in enumerate(cells):
                    for b in range(NB):
                        par = b % 2
                        if k == 0:
                            written, n = xn_ready, h * NB + (b + 1)
                        else:
                            written, n = evac_done, h * OH + (outs_before[k - 1] + (b + 1) * len(cells[k - 1][2]))
                        if b >= 2:
                            wait_both(written, n, lo_ready, h * TH + (tiles_before[k] + (b - 1) * (len(ins) + 1)))
                        elif k:
                            before = tiles_before[k] - (1 - b) * (len(cells[k - 1][1]) + 1)
                            wait_both(written, n, lo_ready, h * TH + before)
                        else:
                            sp.wait_ge(written, n)
                        for g, s in enumerate(ins):
                            at = HALO * g
                            sp.dma_start(HS[at:at + C, par, 1:YB, 1:WD + 1],
                                         SV[P - C:P, s, b, 0:YB - 1, :]).then_inc(halo_loaded[par], 16)
                            sp.dma_start(HS[at + C:at + HALO, par, 0:YB - 1, 1:WD + 1],
                                         SV[0:C, s, b, 1:YB, :]).then_inc(halo_loaded[par], 16)
                        if b == 0 and k + 2 < NC:
                            wait_both(win_hi, h * NC + (k + 2), win_lo, h * NC + (k + 2))
                            load_taps(k + 2)
                wait_both(win_hi, h * NC + NC, win_lo, h * NC + NC)
                load_taps(0)
            sp.wait_ge(taps_loaded, (FILL_AT[0] + 1) * 16)
            sp.dma_start(RAW[0:C, 0:C * 9], l1w.rearrange("o i k d -> o (i k d)")).then_inc(taps_loaded, 16)

            def halo_block(blk, par):
                src = NS1[par] if blk == 1 else NS[par]
                dst = H1[par] if blk == 1 else HS[:, par]
                for g in range(3 if blk == 2 else 1):
                    top, bot = HALO * g, HALO * g + C
                    sp.dma_start(dst[top:top + C, 1:YB], src[P - C:P, 0:YB - 1])\
                      .then_inc(halo_loaded[par], 16)
                    sp.dma_start(dst[bot:bot + C, 0:YB - 1], src[0:C, 1:YB])\
                      .then_inc(halo_loaded[par], 16)
                if blk == 1:
                    sp.dma_start(dst[0:C, 0:1], src[P - C:P, YB - 1:YB]).then_inc(halo_loaded[par], 16)
                    sp.dma_start(dst[C:HALO, YB - 1:YB], src[0:C, 0:1]).then_inc(halo_loaded[par], 16)

            ov = out.rearrange("b c (yb yi) w -> b yi c yb w", yi=YI)

            for blk in (1, 2):
                if blk == 2:
                    sp.wait_ge(win_hi, FILL_AT[0] + 1)
                    sp.wait_ge(win_lo, FILL_AT[0] + 1)
                    sp.dma_start(RAW[0:C, 0:C * 9], l3w).then_inc(taps_loaded, 16)
                n = TILES_OF[blk]
                before = TILES_OF.get(blk - 1, 2)
                for b in range(2):
                    sp.wait_ge(xn_ready, blk * B + (b + 1))
                    sp.wait_ge(lo_ready, T_AT[blk - 1] - (1 - b) * before)
                    halo_block(blk, b)
                with sp.Fori(1, B // 2) as i:
                    for par in range(2):
                        wait_both(xn_ready, i * 2 + (blk * B + par + 1),
                                  lo_ready, i * (2 * n) + (T_AT[blk - 1] + (par - 1) * n))
                        halo_block(blk, par)

            for b in range(B + 2):
                if b < B:
                    sp.wait_ge(xn_ready, 3 * B + b + 1)
                    sp.wait_ge(lo_ready, T_AT[2] + (b - 1) * 2 if b > 1 else T_AT[2] - (1 - b) * PER)
                    halo_block(3, b % 2)
                if b >= 2:
                    sp.wait_ge(out_staged, b - 1)
                    for yi in range(YI):
                        sp.dma_start(ov[b - 2, yi], XV[C * yi:C * (yi + 1), b - 2]).then_inc(stored, 16)
            sp.wait_ge(stored, B * YI * 16)

        @block.gpsimd
        def _(pool):
            pool.memset(NHALF[:, :], -0.5).then_inc(pool_const, 1)
            for par in range(2):
                for part in range(2):
                    last = pool.memset(W[0:3 * HALO, par, part, MAIN_TILES:TILES, :].bitcast(F32), 0.0)
            last.then_inc(w_clear, 1)
            pool.wait_ge(pool_const, 1)

            def norm(cols, images, n):
                pool.wait_ge(nv_ready, n)
                pass_wait(pool, passed["pool"])
                pool.tensor_tensor(RS[:, images], VE[:, cols], NHALF[:, cols], ALU.pow).then_inc(pool_norm, 1)
                pool.wait_ge(pool_norm, n)
                pass_wait(pool, passed["pool"])
                pool.tensor_tensor(NBI[:, images], GM[:, cols, 0], RS[:, images], ALU.mult).then_inc(norm_ready, 1)

            norm(slice(0, B), slice(0, B), 1)

            NJ = 4
            o0 = 2 * NB * PIX
            o1 = o0 + NJ * 81 * BASES
            o2 = o1 + NJ * 81
            SPL = flat[0:C, o0:o1].rearrange("o (j a n s) -> o j a n s", j=NJ, a=9, n=9)
            SPF = flat[0:C, o0:o1].rearrange("o (q s) -> o q s", s=BASES)
            SCL = flat[0:C, o1:o2]
            BAS = flat[0:C, o2:o2 + NJ * 81]
            BAV = BAS.rearrange("o (j a n) -> o j a n", j=NJ, a=9)
            SUM = SPF.rearrange("o (j a n) s -> o j a (n s)", j=NJ, a=9)
            steps = 0
            for c in range(C // NJ):
                js = slice(c * NJ, (c + 1) * NJ)
                pool.dma_start(flat[0:C, o0:o1],
                               l2spline[:, js].rearrange("o j a n s -> o (j a n s)")).then_inc(kan_loaded, 16)
                pool.dma_start(SCL, l2scale[:, js].rearrange("o j a n -> o (j a n)")).then_inc(kan_loaded, 16)
                pool.dma_start(BAS, l2base[:, js].rearrange("o j a n -> o (j a n)")).then_inc(kan_loaded, 16)
                pool.wait_ge(kan_loaded, 48 * (c + 1))
                scl = SCL.rearrange("o (q s) -> o q s", s=1).broadcast_to([C, NJ * 81, BASES])
                pool.tensor_tensor(SPF, SPF, scl, ALU.mult).then_inc(pool_step, 1)
                steps += 1
                for a in range(1, 9):
                    pool.wait_ge(pool_step, steps)
                    pool.tensor_tensor(SUM[:, :, 0], SUM[:, :, 0], SUM[:, :, a], ALU.add).then_inc(pool_step, 1)
                    pool.tensor_tensor(BAV[:, :, 0], BAV[:, :, 0], BAV[:, :, a], ALU.add).then_inc(pool_step, 1)
                    steps += 2
                pool.wait_ge(pool_step, steps)
                pool.tensor_scalar(KAN[:, 0:BASES, js, :].rearrange("o s j n -> o j n s"), SPL[:, :, 0],
                                   -1.0 / 6.0, None, ALU.mult).then_inc(kan_chunk, 1)
                pool.tensor_copy(KAN[:, BASES, js, :], BAV[:, :, 0]).then_inc(kan_chunk, 1)
                pool.wait_ge(kan_chunk, 2 * (c + 1))

            for blk in range(2):
                with pool.Fori(0, B // 2) as i:
                    for par in range(2):
                        norm(slice(par, par + 1), bass.ds(i * 2 + par, 1), i * 2 + (2 + par + blk * B))
            nb = 0
            for first in (True, False):
                with (ExitStack() if first else pool.Fori(1, B // 2)) as i:
                    i = 0 if first else i
                    k = 0
                    for e, (par, t) in enumerate(ENTRIES):
                        if e == 11 and not first:
                            norm(slice(1, 2), bass.ds(i * 2 - 1, 1), i * 2 + (2 + 2 * B - 1))
                        if e == 23:
                            norm(slice(0, 1), bass.ds(i * 2, 1), i * 2 + (2 + 2 * B))
                        if t == BASES:
                            continue
                        k += 1
                        pt = basis_parts(t)
                        pool.wait_ge(basis_b, i * BASES_PER_PAIR + k)
                        pool.tensor_tensor(TB[e % 3][0:pt], TB[e % 3][0:pt], B2[e % 3][0:pt], ALU.mult)\
                            .then_inc(basis_b3, 1)
            norm(slice(1, 2), slice(B - 1, B), 2 + 3 * B - 1)

        def basis_act(act, normalise):
            for first in (True, False):
                with (ExitStack() if first else act.Fori(1, B // 2)) as i:
                    i = 0 if first else i
                    if first:
                        act.wait_ge(out_done, O_AT[3])
                    for par in range(2):
                        b = i * 2 + par
                        normalise(NS[par][:, :, 1:WD + 1], b, b + (2 + B)).then_inc(xn_ready, 1)
                    act.wait_ge(xn_ready, i * 2 + (2 * B + 2))
                    base_u = i * ENTRIES_PER_PAIR
                    nb = 0
                    for e in range(ENTRIES_PER_PAIR + 2):
                        if e < ENTRIES_PER_PAIR:
                            par, t = ENTRIES[e]
                            src, parts = NS[par], P
                            if t > BASES:
                                src, parts = HS[:, par], 3 * HALO
                            if t == BASES + 1:
                                act.wait_ge(halo_loaded[par], i * 96 + (H_AT[1] + 96))
                            if e >= 3:
                                act.wait_ge(feat_ready, base_u + (e - 2))
                            elif not first:
                                act.wait_ge(feat_ready, base_u)
                            u, tb, b2 = UA[e % 3], TB[e % 3], B2[e % 3]
                            pt = basis_parts(t)
                            if pt:
                                col = t if t < BASES else t - 1
                                last = act.activation(u[0:pt], src[0:pt], ACT.Abs, scale=2.5,
                                                      bias=CB[0:pt, col:col + 1])
                            if pt < parts:
                                last = act.activation(u[pt:parts], src[pt:parts], ACT.Tanh, scale=0.5)
                            last.then_inc(basis_u, 1)
                            if pt:
                                nb += 1
                                act.wait_ge(basis_u, base_u + (e + 1))
                                act.activation(tb[0:pt], u[0:pt], ACT.Relu, scale=-1.0, bias=1.0)\
                                   .then_inc(act_step, 1)
                                act.wait_ge(act_step, i * BASES_PER_PAIR + nb)
                                act.activation(b2[0:pt], tb[0:pt], ACT.Square).then_inc(basis_b, 1)
                        if e >= 2:
                            q = e - 2
                            par, t = ENTRIES[q]
                            parts = P if t <= BASES else 3 * HALO
                            if not (first and q < FSLOTS):
                                act.wait_ge(tile_used, base_u + (q + 1 - FSLOTS))
                            act.wait_ge(feat_ready, base_u + (q + 1))
                            act.activation(F[0:parts, q % FSLOTS, 0], FT[q % 3][0:parts], ACT.Copy)\
                               .then_inc(hi_ready, 1)

        @block.scalar
        def _(act):
            xv = x.rearrange("b c (yb yi) w -> b yi c yb w", yi=YI)
            for b in range(B):
                for yi in range(1, YI, 2):
                    act.dma_start(XV[C * yi:C * (yi + 1), b], xv[b, yi]).then_inc(x_loaded, 16)
            act.wait_ge(const_loaded, 96)
            act.activation(ID[:, :], IDF[:, :], ACT.Copy).then_inc(id_ready, 1)

            def fill(kind, g0, n, prev_chunks, n_taps):
                if kind == "kan":
                    act.wait_ge(kan_chunk, 2 * (C // 4))
                else:
                    act.wait_ge(taps_loaded, n_taps)
                if prev_chunks is not None:
                    act.wait_ge(chunk_lo, prev_chunks)
                fill_windows(nc.scalar, 0, kind, g0, n, win_hi)

            def banded(chunks, parity, h, at):
                for c, (kind, q, base, n_out) in enumerate(chunks):
                    act.wait_ge(chunk_hi, at_half(h, CH, at + c + 1))
                    bank = BUILD_HI[(at + c) % 2]
                    dst, src = weight_dest(0, parity, kind, base, n_out, q), source(bank, kind, n_out)
                    if kind == "main":
                        act.activation(dst, src, ACT.Copy).then_inc(w_hi, 1)
                    else:
                        act.activation(dst[:, 0], src, ACT.Copy, scale=MASK[0:3 * HALO, 0:1])
                        act.activation(dst[:, 1], src, ACT.Copy, scale=MASK[0:3 * HALO, 1:2]).then_inc(w_hi, 1)

            def normalise(dst, b, n):
                act.wait_ge(norm_ready, n)
                return act.activation(dst, ximg(b), ACT.Identity, bias=NBI[:, bass.ds(b, 1)],
                                      scale=RS[:, bass.ds(b, 1)])

            def split_hi(h, k, b):
                ins = cells[k][1]
                par = b % 2
                if k == 0:
                    act.wait_ge(xn_ready, h * NB + (b + 1))
                else:
                    act.wait_ge(evac_done, h * OH + (outs_before[k - 1] + (b + 1) * len(cells[k - 1][2])))
                if b >= 2:
                    act.wait_ge(out_done, h * OH + (outs_before[k] + (b - 1) * len(cells[k][2])))
                elif k:
                    act.wait_ge(out_done, h * OH + (outs_before[k] - (1 - b) * len(cells[k - 1][2])))
                for g, s in enumerate(ins):
                    act.activation(F[:, par * 4 + g, 0, :, 1:WD + 1], SV[:, s, b], ACT.Copy)\
                       .then_inc(hi_ready, 1)
                n = len(ins)
                loads = halo_before[k] + (b // 2 + 1) * 2 * n * 16
                act.wait_ge(halo_loaded[par], h * HH + loads)
                act.activation(F[0:HALO * n, par * 4 + n, 0, :, 1:WD + 1],
                               HS[0:HALO * n, par, :, 1:WD + 1], ACT.Copy).then_inc(hi_ready, 1)

            act.wait_ge(f_clear, 1)
            act.wait_ge(win_clear, 1)
            act.wait_ge(w_clear, 1)
            with act.Fori(0, HALVES) as h:
                fill("cell", 0, NG, None, h * (NC * 16) + 16)
                for b in range(NB):
                    normalise(SV[:, 0, b], h * NB + b, 1).then_inc(xn_ready, 1)
                banded(CELL_FILL[0], 0, h, 0)
                split_hi(h, 0, 0)
                fill("cell", 0, NG, h * CH + chunks_before[1], h * (NC * 16) + 32)
                for k, (cell, ins, outs) in enumerate(cells):
                    if k + 1 < NC:
                        banded(CELL_FILL[k + 1], (k + 1) % 2, h, chunks_before[k + 1])
                    if k == 2:
                        act.wait_ge(kan_chunk, 2 * (C // 4))
                    for b in range(NB):
                        if b + 1 < NB:
                            split_hi(h, k, b + 1)
                        elif k + 1 < NC:
                            split_hi(h, k + 1, 0)
                        for o, (group, slot) in enumerate(outs):
                            act.wait_ge(out_done, h * OH + (outs_before[k] + b * len(outs) + o + 1))
                            act.activation(S[:, slot, b], out_bank(outs, o, b)[:, :], ACT.Relu,
                                           bias=BIAS[:, cell * NG + group:cell * NG + group + 1])\
                               .then_inc(evac_done, 1)
                        if b == 1 and k + 2 < NC:
                            fill("cell", 0, NG, h * CH + chunks_before[k + 2],
                                 h * (NC * 16) + 16 * (k + 3))

            fill("circular", 0, 1, C_AT[0], (FILL_AT[0] + 2) * 16)
            banded(FILL1, 0, None, C_AT[0])
            for t in range(3):
                fill("kan", 3 * t, 3, C_AT[1] + 12 * t, None)
                banded(FILL2[t], 1, None, C_AT[1] + 12 * t)

            def split_block(blk, i, par):
                b = i * 2 + par
                dst = NS1[par] if blk == 1 else NS[par]
                n = b + (2 + (blk - 1) * B)
                last = normalise(dst[:, :, 1:WD + 1], b, n)
                if blk == 1:
                    for col, src in ((0, WD - 1), (WD + 1, 0)):
                        last = act.activation(dst[:, :, col:col + 1], ximg(b)[:, :, src:src + 1], ACT.Identity,
                                              bias=NBI[:, bass.ds(b, 1)], scale=RS[:, bass.ds(b, 1)])
                last.then_inc(xn_ready, 1)
                act.wait_ge(xn_ready, b + (blk * B + 1))
                act.activation(F[:, par * 4, 0], dst, ACT.Copy).then_inc(hi_ready, 1)
                halo = H1[par] if blk == 1 else HS[:, par]
                per = (4 if blk == 1 else 2) * 16
                act.wait_ge(halo_loaded[par], i * per + (H_AT[blk - 1] + per))
                act.activation(F[0:HALO, par * 4 + 1, 0], halo[0:HALO], ACT.Copy).then_inc(hi_ready, 1)

            act.wait_ge(scratch_clear, 1)
            for blk in (1, 2, 3):
                if blk == 2:
                    fill("conv", 0, 1, C_AT[2], (FILL_AT[0] + 3) * 16)
                    banded(FILL1, 0, None, C_AT[2])
                    basis_act(act, normalise)
                    continue
                for b in range(2):
                    if blk == 1:
                        act.wait_ge(out_done, O_AT[1])
                    else:
                        act.wait_ge(tile_used, PER * B)
                    split_block(blk, 0, b)
                with act.Fori(1, B // 2) as i:
                    for par in range(2):
                        act.wait_ge(out_done, i * 2 + (O_AT[blk] + par - 1))
                        split_block(blk, i, par)

        @block.vector
        def _(dve):
            steps = Count()

            nc.vector.memset(WIN_T[:, :, :, :].bitcast(F32), 0.0).then_inc(win_clear, 1)
            nc.vector.memset(HS[:, :, :, :], 0.0).then_inc(hs_clear, 1)
            edges = F[:, :, :, :, :].bitcast(F32).rearrange("p s a y w -> p (s a y) w")
            for col in (0, WD + 1):
                last = nc.vector.memset(edges[:, :, col:col + 1], 0.0)
            last.then_inc(f_clear, 1)

            dve.wait_ge(const_loaded, 96)
            for yi in range(YI):
                nc.vector.tensor_copy(BN_REP[:, yi], BN_IN[:, :])
                last = nc.vector.tensor_copy(OB_REP[:, yi], OB_IN[:, :])
            last.then_inc(bias_rep, 1)

            dve.wait_ge(x_loaded, 16 * YI * B)
            for b in range(B):
                last = nc.vector.bn_stats(STATS[:, b], X[:, b])
            last.then_inc(dve_step, 1)
            dve.wait_ge(dve_step, steps.next())
            for b in range(B):
                last = nc.vector.bn_aggr(MV[:, b], STATS[:, b])
            last.then_inc(dve_step, 1)
            dve.wait_ge(dve_step, steps.next())

            def squares(cols):
                m, v = MV[:, cols, 0], MV[:, cols, 1]
                nc.vector.tensor_tensor(NV[:, cols], m, m, ALU.mult).then_inc(dve_step, 1)
                dve.wait_ge(dve_step, steps.next())
                nc.vector.scalar_tensor_tensor(v, v, GN_EPS, NV[:, cols], ALU.add, ALU.add).then_inc(mv_ready, 1)

            def group_stats(cols, bank, n):
                dve.wait_ge(group_ready, n)
                g = GM[:, cols, :].rearrange("p b a -> p (b a)")
                nc.vector.tensor_scalar(g, bank[:, 2 * cols.start:2 * cols.stop], -1.0, None, ALU.mult)\
                    .then_inc(dve_step, 1)
                dve.wait_ge(dve_step, steps.next())
                m, v = GM[:, cols, 0], GM[:, cols, 1]
                nc.vector.tensor_tensor(NV[:, cols], m, m, ALU.mult).then_inc(dve_step, 1)
                dve.wait_ge(dve_step, steps.next())
                nc.vector.scalar_tensor_tensor(VE[:, cols], NV[:, cols], -1.0, v, ALU.mult, ALU.subtract)\
                    .then_inc(nv_ready, 1)

            def image_stats(b, par):
                nc.vector.bn_stats(STATS[:, par], ximg_flat(b)).then_inc(dve_step, 1)
                dve.wait_ge(dve_step, steps.next())
                pass_wait(dve, passed["dve"])
                nc.vector.bn_aggr(MV[:, par], STATS[:, par]).then_inc(dve_step, 1)
                dve.wait_ge(dve_step, steps.next())
                squares(slice(par, par + 1))

            squares(slice(0, B))
            group_stats(slice(0, B), STAT_BANK[0], 1)
            dve.wait_ge(bias_done, 1)
            nc.vector.tensor_copy(BIAS[:, :], OUT_BANK[0][:, 0:NG * C])
            nc.vector.tensor_copy(OB[:, :], OUT_BANK[0][:, 64:66]).then_inc(bias_ready, 1)

            def fill(kind, g0, n, n_hi):
                dve.wait_ge(win_hi, n_hi)
                fill_windows(nc.vector, 1, kind, g0, n, win_lo)

            def banded(chunks, parity, h, at):
                for c, (kind, q, base, n_out) in enumerate(chunks):
                    dve.wait_ge(chunk_lo, at_half(h, CH, at + c + 1))
                    bank = BUILD_LO[(at + c) % 2]
                    dst, src = weight_dest(1, parity, kind, base, n_out, q), source(bank, kind, n_out)
                    if kind == "main":
                        nc.vector.tensor_copy(dst, src).then_inc(w_lo, 1)
                    else:
                        nc.vector.tensor_scalar(dst[:, 0], src, MASK[0:3 * HALO, 0:1], None, ALU.mult)
                        nc.vector.tensor_scalar(dst[:, 1], src, MASK[0:3 * HALO, 1:2], None, ALU.mult)\
                            .then_inc(w_lo, 1)

            def split_lo(h, k, b):
                ins = cells[k][1]
                par, n = b % 2, len(ins)
                at = tiles_before[k] + b * (n + 1)
                for g, s in enumerate(ins):
                    dve.wait_ge(hi_ready, h * TH + (at + g + 1))
                    nc.vector.tensor_tensor(F[:, par * 4 + g, 1, :, 1:WD + 1], SV[:, s, b],
                                            F[:, par * 4 + g, 0, :, 1:WD + 1].bitcast(F32), ALU.subtract)\
                        .then_inc(lo_ready, 1)
                dve.wait_ge(hi_ready, h * TH + (at + n + 1))
                rows = slice(0, HALO * n)
                nc.vector.tensor_tensor(F[rows, par * 4 + n, 1, :, 1:WD + 1], HS[rows, par, :, 1:WD + 1],
                                        F[rows, par * 4 + n, 0, :, 1:WD + 1].bitcast(F32), ALU.subtract)\
                    .then_inc(lo_ready, 1)

            def tail(b, par, blk):
                dve.wait_ge(norm_ready, b + (1 + blk * B))
                group_stats(slice(par, par + 1), STAT_BANK[par], b + (2 + blk * B))

            half_links = NB * LINKS_PER_IMAGE
            links0 = steps.n + steps.base
            with dve.Fori(0, HALVES) as h:
                steps.enter(h * half_links + links0)
                fill("cell", 0, NG, h * NC + 1)
                banded(CELL_FILL[0], 0, h, 0)
                split_lo(h, 0, 0)
                fill("cell", 0, NG, h * NC + 2)
                for k, (cell, ins, outs) in enumerate(cells):
                    if k + 1 < NC:
                        banded(CELL_FILL[k + 1], (k + 1) % 2, h, chunks_before[k + 1])
                    for b in range(NB):
                        if b + 1 < NB:
                            split_lo(h, k, b + 1)
                        elif k + 1 < NC:
                            split_lo(h, k + 1, 0)
                        if b == 1 and k + 2 < NC:
                            fill("cell", 0, NG, h * NC + (k + 3))
                        if k == NC - 1:
                            img = h * NB + b
                            dve.wait_ge(evac_done, h * OH + (outs_before[k] + b + 1))
                            nc.vector.tensor_tensor(ximg_flat(img), ximg_flat(img), S[:, outs[0][1], b], ALU.add)\
                                .then_inc(added, 1)
                            dve.wait_ge(added, img + 1)
                            pass_wait(dve, passed["dve"])
                            image_stats(img, b % 2)
                            if b:
                                tail(h * NB + (b - 1), (b - 1) % 2, 0)
                tail(h * NB + (NB - 1), (NB - 1) % 2, 0)
                assert steps.n == half_links
            steps.enter(links0 + HALVES * half_links)

            for par in range(2):
                for col in (0, WD + 1):
                    last = nc.vector.memset(NS[par][:, :, col:col + 1], 0.0)
            last.then_inc(scratch_clear, 1)

            fill("circular", 0, 1, FILL_AT[0] + 1)
            banded(FILL1, 0, None, C_AT[0])
            for t in range(3):
                fill("kan", 3 * t, 3, FILL_AT[1] + t + 1)
                banded(FILL2[t], 1, None, C_AT[1] + 12 * t)

            def split_block(blk, b, par):
                src = NS1[par] if blk == 1 else NS[par]
                halo = H1[par] if blk == 1 else HS[:, par]
                dve.wait_ge(hi_ready, b * 2 + (T_AT[blk - 1] + 1))
                nc.vector.tensor_tensor(F[:, par * 4, 1], src, F[:, par * 4, 0].bitcast(F32), ALU.subtract)\
                    .then_inc(lo_ready, 1)
                dve.wait_ge(hi_ready, b * 2 + (T_AT[blk - 1] + 2))
                nc.vector.tensor_tensor(F[0:HALO, par * 4 + 1, 1], halo[0:HALO],
                                        F[0:HALO, par * 4 + 1, 0].bitcast(F32), ALU.subtract)\
                    .then_inc(lo_ready, 1)

            def update(blk, b, par):
                if blk == 2:
                    dve.wait_ge(tile_used, b * PER + PER)
                else:
                    dve.wait_ge(out_done, b + (O_AT[blk] + 1))
                psum, ximage = OUT_BANK[par][:, :], ximg_flat(b)
                if blk == 1:
                    nc.vector.tensor_tensor(ximage, psum, ximage, ALU.add).then_inc(added, 1)
                elif blk == 2:
                    nc.vector.scalar_tensor_tensor(ximage, psum, OB[:, 0:1], ximage, ALU.add, ALU.add)\
                        .then_inc(added, 1)
                else:
                    nc.vector.scalar_tensor_tensor(ximage, psum, OB[:, 1:2], ximage, ALU.add, ALU.add)\
                        .then_inc(out_staged, 1)
                if blk < 3:
                    dve.wait_ge(added, b + (blk * B + 1))
                    pass_wait(dve, passed["dve"])
                    image_stats(b, par)

            split_block(1, 0, 0)
            split_block(1, 1, 1)
            update(1, 0, 0)
            links1 = steps.n + steps.base
            with dve.Fori(1, B // 2) as i:
                steps.enter((i - 1) * (2 * LINKS_PER_IMAGE) + links1)
                for par in range(2):
                    split_block(1, i * 2 + par, par)
                    update(1, i * 2 + (par - 1), 1 - par)
                    tail(i * 2 + (par - 2), par, 1)
                assert steps.n == 2 * LINKS_PER_IMAGE
            steps.enter(links1 + (B // 2 - 1) * 2 * LINKS_PER_IMAGE)
            update(1, B - 1, 1)
            tail(B - 2, 0, 1)
            tail(B - 1, 1, 1)

            fill("conv", 0, 1, FILL_AT[2] + 1)
            banded(FILL1, 0, None, C_AT[2])

            for first in (True, False):
                if not first:
                    links2 = steps.n + steps.base
                with (ExitStack() if first else dve.Fori(1, B // 2)) as i:
                    if first:
                        i = 0
                    else:
                        steps.enter((i - 1) * PAIR_LINKS + links2)
                    base_u = i * ENTRIES_PER_PAIR
                    base_b = i * BASES_PER_PAIR
                    nb = 0
                    counts = {}
                    for e in range(ENTRIES_PER_PAIR + 3):
                        if e < ENTRIES_PER_PAIR:
                            par, t = ENTRIES[e]
                            pt = basis_parts(t)
                            parts = P if t <= BASES else 3 * HALO
                            u, a, a2 = UA[e % 3], TA[e % 3], A2[e % 2]
                            dve.wait_ge(basis_u, base_u + (e + 1))
                            if pt:
                                nb += 1
                                counts[e] = nb
                                nc.vector.tensor_scalar(a[0:pt], u[0:pt], 2.0, 2.0, ALU.min, ALU.subtract)\
                                    .then_inc(dve_step, 1)
                                dve.wait_ge(dve_step, steps.next())
                                nc.vector.tensor_tensor(a2[0:pt], a[0:pt], a[0:pt], ALU.mult).then_inc(dve_step, 1)
                                dve.wait_ge(dve_step, steps.next())
                                nc.vector.tensor_tensor(a2[0:pt], a2[0:pt], a[0:pt], ALU.mult).then_inc(dve_step, 1)
                                dve.wait_ge(dve_step, steps.next())
                            if pt < parts:
                                nc.vector.tensor_scalar(a[pt:parts], u[pt:parts], 0.5, 0.5, ALU.mult, ALU.add)\
                                    .then_inc(dve_step, 1)
                                dve.wait_ge(dve_step, steps.next())
                        if 1 <= e <= ENTRIES_PER_PAIR:
                            q = e - 1
                            par, t = ENTRIES[q]
                            pt = basis_parts(t)
                            parts = P if t <= BASES else 3 * HALO
                            src = NS[par] if t <= BASES else HS[:, par]
                            if pt < parts:
                                last = nc.vector.tensor_tensor(FT[q % 3][pt:parts], TA[q % 3][pt:parts],
                                                               src[pt:parts], ALU.mult)
                            if pt:
                                dve.wait_ge(basis_b3, base_b + counts[q])
                                last = nc.vector.scalar_tensor_tensor(
                                    flat2(FT[q % 3])[0:pt], flat2(TB[q % 3])[0:pt], 4.0,
                                    flat2(A2[q % 2])[0:pt], ALU.mult, ALU.add)
                            last.then_inc(feat_ready, 1)
                        if e >= 3:
                            q = e - 3
                            par, t = ENTRIES[q]
                            parts = P if t <= BASES else 3 * HALO
                            dve.wait_ge(feat_ready, base_u + (q + 1))
                            dve.wait_ge(hi_ready, base_u + (T_AT[1] + q + 1))
                            nc.vector.tensor_tensor(F[0:parts, q % FSLOTS, 1], FT[q % 3][0:parts],
                                                    F[0:parts, q % FSLOTS, 0].bitcast(F32), ALU.subtract)\
                                .then_inc(lo_ready, 1)
                        if e == 5 and not first:
                            update(2, i * 2 - 1, 1)
                        if e == 11 and not first:
                            tail(i * 2 - 1, 1, 2)
                        if e == 17:
                            update(2, i * 2, 0)
                        if e == 23:
                            tail(i * 2, 0, 2)
                    if not first:
                        assert steps.n == PAIR_LINKS
            steps.enter(links2 + (B // 2 - 1) * PAIR_LINKS)
            update(2, B - 1, 1)
            tail(B - 1, 1, 2)

            split_block(3, 0, 0)
            split_block(3, 1, 1)
            update(3, 0, 0)
            with dve.Fori(1, B // 2) as i:
                for par in range(2):
                    split_block(3, i * 2 + par, par)
                    update(3, i * 2 + (par - 1), 1 - par)
            update(3, B - 1, 1)

        @block.tensor
        def _(pe):
            pe.wait_ge(const_loaded, 96)
            pe.wait_ge(bias_rep, 1)
            nc.tensor.matmul(OUT_BANK[0][:, 0:NG * C], BN_REP[:, :, :].rearrange("k y c -> k (y c)"), IDF[:, :],
                             start=True, stop=True)
            nc.tensor.matmul(OUT_BANK[0][:, 64:66], OB_REP[:, :, :].rearrange("k y c -> k (y c)"), IDF[0:2, 0:2],
                             start=True, stop=True).then_inc(bias_done, 1)
            pe.wait_ge(mv_ready, 1)
            nc.tensor.matmul(STAT_BANK[0][:, 0:2 * B], G[:, :], MV[:, :, :].rearrange("p b a -> p (b a)"),
                             start=True, stop=True).then_inc(group_ready, 1)

            def group_means(par, n):
                pe.wait_ge(mv_ready, n)
                nc.tensor.matmul(STAT_BANK[par][:, 2 * par:2 * par + 2], G[:, :], MV[:, par, :],
                                 start=True, stop=True).then_inc(group_ready, 1)

            def build_banded(chunks, co, h, at, n_fill):
                pe.wait_ge(win_hi, n_fill)
                pe.wait_ge(win_lo, n_fill)
                for c, (kind, q, _, n_out) in enumerate(chunks):
                    cc = at + c
                    for part, banks, free, built in ((0, BUILD_HI, w_hi, chunk_hi), (1, BUILD_LO, w_lo, chunk_lo)):
                        if h is None or cc >= 2:
                            pe.wait_ge(free, at_half(h, CH, cc - 1))
                        bank = banks[cc % 2]
                        if kind == "main":
                            for j in range(YI):
                                s = LEAD + q * TAP_SLOTS - j + 1
                                last = nc.tensor.matmul(
                                    bank[:, j * co:(j + 1) * co],
                                    WIN_T[0:co, part, s:s + YI, :].rearrange("o s c -> o (s c)"),
                                    ID[0:co, 0:co], start=True, stop=True)
                        else:
                            last = nc.tensor.matmul(bank[0:3 * HALO, 0:co],
                                                    WH[0:co, part, q].rearrange("o s c -> o (s c)"),
                                                    ID[0:co, 0:co], start=True, stop=True)
                        last.then_inc(built, 1)

            PRODUCTS = ((0, 0), (0, 1), (1, 0))

            def convolve(bank, parity, terms, open_, close):
                todo = [(tile + dx * step, slot, rows, dx, wp, fp) for tile, step, slot, rows in terms
                        for dx in range(K3) for wp, fp in PRODUCTS]
                for n, (tile, slot, rows, dx, wp, fp) in enumerate(todo):
                    last = nc.tensor.matmul(bank[:, :].rearrange("p (y x) -> p y x", x=WD),
                                            W[0:rows, parity, wp, tile, :], F[0:rows, slot, fp, :, dx:dx + WD],
                                            start=open_ and n == 0, stop=close and n == len(todo) - 1)
                return last

            def cell_step(h, k, b, par):
                _, ins, outs = cells[k]
                n, m = len(ins), len(outs)
                if par == 0:
                    pe.wait_ge(w_hi, h * CH + chunks_before[k + 1])
                    pe.wait_ge(w_lo, h * CH + chunks_before[k + 1])
                    if k:
                        pe.wait_ge(evac_done, h * OH + outs_before[k])
                at = b * (n + 1) + (tiles_before[k] + n + 1)
                pe.wait_ge(hi_ready, h * TH + at)
                pe.wait_ge(lo_ready, h * TH + at)
                for o, (group, _) in enumerate(outs):
                    if m > 1:
                        if not (k == 0 and isinstance(b, int) and b == 0):
                            pe.wait_ge(evac_done, h * OH + (b * m + (outs_before[k] - m + o + 1)))
                    elif not (k == 0 and isinstance(b, int) and b < 2):
                        pe.wait_ge(evac_done, h * OH + (b + (outs_before[k] - 1)))
                    terms = [(g * K3 * NG + group, NG, par * 4 + g, P) for g in range(n)]
                    terms.append((MAIN_TILES + group, NG, par * 4 + n, HALO * n))
                    convolve(out_bank(outs, o, par), k % 2, terms, True, True).then_inc(out_done, 1)

            pe.wait_ge(id_ready, 1)
            pe.wait_ge(bias_ready, 1)
            with pe.Fori(0, HALVES) as h:
                build_banded(CELL_FILL[0], NG * C, h, 0, h * NC + 1)
                for k, (_, ins, outs) in enumerate(cells):
                    if k + 1 < NC:
                        build_banded(CELL_FILL[k + 1], NG * C, h, chunks_before[k + 1], h * NC + (k + 2))
                    if k == 0:
                        for b in range(NB):
                            cell_step(h, k, b, b % 2)
                    elif k < NC - 1:
                        with pe.Fori(0, NB // 2) as i:
                            for par in range(2):
                                cell_step(h, k, i * 2 + par, par)
                    else:
                        for b in range(NB):
                            cell_step(h, k, b, b % 2)
                            if b:
                                img = h * NB + (b - 1)
                                group_means((b - 1) % 2, img + 2)
                        img = h * NB + (NB - 1)
                        group_means((NB - 1) % 2, img + 2)

            build_banded(FILL1, C, None, C_AT[0], FILL_AT[0] + 1)
            for t in range(3):
                build_banded(FILL2[t], C, None, C_AT[1] + 12 * t, FILL_AT[1] + t + 1)

            def block_step(blk, b, par):
                pe.wait_ge(hi_ready, b * 2 + (T_AT[blk - 1] + 2))
                pe.wait_ge(lo_ready, b * 2 + (T_AT[blk - 1] + 2))
                convolve(OUT_BANK[par], 0, [(0, 1, par * 4, P), (MAIN_TILES, 1, par * 4 + 1, HALO)], True, True)\
                    .then_inc(out_done, 1)

            pe.wait_ge(w_hi, C_AT[1])
            pe.wait_ge(w_lo, C_AT[1])
            pe.wait_ge(evac_done, HALVES * OH)
            block_step(1, 0, 0)
            block_step(1, 1, 1)
            group_means(0, 2 + B)
            with pe.Fori(1, B // 2) as i:
                for par in range(2):
                    pe.wait_ge(added, i * 2 + (B + par - 1))
                    block_step(1, i * 2 + par, par)
                    group_means(1 - par, i * 2 + (par - 1 + 2 + B))
            group_means(1, 2 + B + B - 1)
            build_banded(FILL1, C, None, C_AT[2], FILL_AT[2] + 1)

            pe.wait_ge(w_hi, C_AT[2])
            pe.wait_ge(w_lo, C_AT[2])
            pe.wait_ge(added, 2 * B)
            for first in (True, False):
                with (ExitStack() if first else pe.Fori(1, B // 2)) as i:
                    i = 0 if first else i
                    for e, (par, t) in enumerate(ENTRIES):
                        if t == 0 and not first:
                            pe.wait_ge(added, i * 2 + (2 * B + par - 1))
                        pe.wait_ge(hi_ready, i * ENTRIES_PER_PAIR + (T_AT[1] + e + 1))
                        pe.wait_ge(lo_ready, i * ENTRIES_PER_PAIR + (T_AT[1] + e + 1))
                        if t <= BASES:
                            term = (t * K3, 1, e % FSLOTS, P)
                        else:
                            term = (MAIN_TILES + (t - FEATS) * K3, 1, e % FSLOTS, 3 * HALO)
                        convolve(OUT_BANK[par], 1, [term], t == 0, t == PER - 1).then_inc(tile_used, 1)
                        if e == 7 and not first:
                            group_means(1, i * 2 + (1 + 2 * B))
                        if e == 19:
                            group_means(0, i * 2 + (2 + 2 * B))
            group_means(1, 1 + 3 * B)

            pe.wait_ge(w_hi, C_AT[2] + 6)
            pe.wait_ge(w_lo, C_AT[2] + 6)
            pe.wait_ge(added, 3 * B)
            block_step(3, 0, 0)
            block_step(3, 1, 1)
            with pe.Fori(1, B // 2) as i:
                for par in range(2):
                    pe.wait_ge(out_staged, i * 2 + (par - 1))
                    block_step(3, i * 2 + par, par)


_INS = ["x", "L0_conv_W", "L0_conv_b", "L1_conv_weight", "L2_conv_base_weight", "L2_conv_spline_weight",
        "L2_conv_spline_scaler", "L2_conv_bias_weight", "L3_conv_combinator", "L3_conv_bias"]


def shape_constants():
    c = np.zeros((P, P + NG * C + 16), np.float32)
    ch = np.arange(P) % C
    c[:, 0:P] = (ch[:, None] // 2 == ch[None, :] // 2) / 16.0
    c[0:NG * C, P:P + NG * C] = np.eye(NG * C)
    at = P + NG * C
    for i in range(BASES):
        c[:, at + i] = 3.5 - i
    for t in range(3):
        c[:, at + BASES + t] = 3.5 - (3 * t + np.arange(P) // HALO)
    for side in range(2):
        c[:, at + BASES + 3 + side] = np.arange(P) // C % 2 == side
    return c


def kernel(**inputs):
    import concourse.bacc as bacc
    from concourse.bass_utils import run_bass_kernel_spmd

    nc = bacc.Bacc("TRN2", target_bir_lowering=False, num_devices=1)
    arrays, args = {}, []
    for name in _INS:
        a = np.ascontiguousarray(inputs[name])
        arrays[f"in_{name}"] = a
        args.append(nc.dram_tensor(f"in_{name}", a.shape, mybir.dt.from_np(a.dtype), kind="ExternalInput").ap())
    consts = shape_constants()
    arrays["in_consts"] = consts
    args.append(nc.dram_tensor("in_consts", consts.shape, mybir.dt.float32, kind="ExternalInput").ap())
    out = nc.dram_tensor("out_0", (B, C, YI * YB, WD), mybir.dt.float32, kind="ExternalOutput").ap()
    build(nc, *args, out)
    r = run_bass_kernel_spmd(nc, [arrays], core_ids=[0])
    return r.results[0]["out_0"]
```

```python
from contextlib import ExitStack

import numpy as np
import concourse.bass as bass
from concourse import mybir

P = 128
C = 16
YI = 8
YB = 8
WD = 64
PW = WD + 2
PIX = YB * WD
B = 8
HALVES = 2
NB = B // HALVES
HALO = 2 * C
K3 = 3
NG = 3
KC = K3 * C
TAP_BLOCKS = 9
CHUNKS = YI + 1
MAIN_TILES = 27
TILES = 36
FSLOTS = 8
BASES = 8
NJ = 2
FEATS = BASES + 1

RIGHT, UP, DOWN = range(3)
GN_EPS = 1e-5


class Count:

    def __init__(self):
        self.base, self.n = 0, 0

    def next(self):
        self.n += 1
        return self.base + self.n

    def enter(self, base):
        self.base, self.n = base, 0


def lattice():
    cells = []
    for col in range(4):
        for row in range(4):
            if col == 0:
                ins = [0] if row == 0 else [3 + row]
            elif row == 0:
                ins = [0, 4]
            elif row == 3:
                ins = [3, 6]
            else:
                ins = [row, 4 + row, 3 + row]
            outs = []
            if col < 3 or row == 3:
                outs.append((RIGHT, row))
            if row > 0 and col < 3:
                outs.append((UP, 3 + row))
            if row < 3:
                outs.append((DOWN, 4 + row))
            cells.append((col * 4 + row, ins, outs))
    return cells


def build(nc, x, l0w, l0b, l1w, l2base, l2spline, l2scale, l2bias, l3w, l3bias, consts, out):
    F32, F32R = mybir.dt.float32, mybir.dt.float32r
    ALU, ACT = mybir.AluOpType, mybir.ActivationFunctionType
    cells = lattice()
    NC = len(cells)

    tiles_before, outs_before, chunks_before, halo_before = [0], [0], [0], [0]
    for _, ins, outs in cells:
        tiles_before.append(tiles_before[-1] + NB * (len(ins) + 1))
        outs_before.append(outs_before[-1] + NB * len(outs))
        chunks_before.append(chunks_before[-1] + CHUNKS)
        halo_before.append(halo_before[-1] + NB // 2 * 2 * len(ins) * 16)
    TH, OH, CH, HH = tiles_before[-1], outs_before[-1], chunks_before[-1], halo_before[-1]
    assert CH % 2 == 0
    T_AT = [HALVES * TH, HALVES * TH + 2 * B, HALVES * TH + 2 * B + 12 * B]
    O_AT = {1: HALVES * OH, 3: HALVES * OH + B}
    C_AT = [HALVES * CH, HALVES * CH + CHUNKS, HALVES * CH + 2 * CHUNKS]
    H_AT = [HALVES * HH, HALVES * HH + B // 2 * 4 * 16, HALVES * HH + B // 2 * 4 * 16 + B // 2 * 6 * 16]
    FILL_AT = [HALVES * NC, HALVES * NC + 1, HALVES * NC + 2]

    ctx = ExitStack()
    with ctx:
        def sb(name, shape, dt=F32):
            return ctx.enter_context(nc.sbuf_tensor(name, shape, dt))

        def sem(name):
            return ctx.enter_context(nc.semaphore(name))

        X = sb("X", [P, B, PIX])
        S = sb("S", [P, 7, NB, PIX])
        F = sb("F", [P, FSLOTS, 2, YB, PW], F32R)
        W = sb("W", [P, 2, 2, TILES, P], F32R)
        HS = sb("HS", [3 * HALO, 2, YB, PW])
        RAW = sb("RAW", [NG * C, NG * C * 9])
        RAWR = sb("RAWR", [NG * C, TAP_BLOCKS, KC])
        WT = sb("WT", [KC, 2, TAP_BLOCKS * NG * C], F32R)
        SEL = sb("SEL", [KC, YI * P + NG * 3 * HALO], F32R)
        KAN = sb("KAN", [C, FEATS * K3, KC])
        G = sb("G", [P, P])
        CB = sb("CB", [P, 16])
        IDF = sb("IDF", [NG * C, NG * C])
        BN_IN = sb("BN_IN", [NG * C, C])
        BN_REP = sb("BN_REP", [NG * C, YI, C])
        BIAS = sb("BIAS", [P, NG * C])
        OB_IN = sb("OB_IN", [2, C])
        OB_REP = sb("OB_REP", [2, YI, C])
        OB = sb("OB", [P, 2])
        STATS = sb("STATS", [P, B, 6])
        MV = sb("MV", [P, B, 2])
        GM = sb("GM", [P, B, 2])
        NV = sb("NV", [P, B])
        VE = sb("VE", [P, B])
        MASK = CB[:, BASES + 3:BASES + 5]
        NHALF = sb("NHALF", [P, B])
        RS = sb("RS", [P, B])
        NBI = sb("NBI", [P, B])

        flat = S[:, :, :, :].rearrange("p a b n -> p (a b n)")
        TS = YB * PW

        def carve(k):
            return flat[:, k * TS:(k + 1) * TS].rearrange("p (y w) -> p y w", w=PW)

        NS1 = [carve(0), carve(1)]
        H1 = [carve(2), carve(3)]
        NS = [carve(4), carve(5)]
        UA = [carve(6 + i) for i in range(3)]
        TA = [carve(9 + i) for i in range(3)]
        TB = [carve(12 + i) for i in range(3)]
        A2 = [carve(15 + i) for i in range(2)]
        B2 = [carve(17 + i) for i in range(3)]
        FT = [carve(20 + i) for i in range(3)]
        assert 23 * TS <= 7 * NB * PIX

        PB = [ctx.enter_context(nc.psum_tensor(f"PB{i}", [P, 512], F32)) for i in range(8)]
        OUT_BANK = PB[0:3]
        BUILD_HI, BUILD_LO = PB[3:5], PB[5:7]
        TR_BANK = PB[7]
        STAT_BANK = [PB[7], PB[2]]
        SEL_IN = flat[0:KC, 6 * NB * PIX:6 * NB * PIX + YI * P + NG * 3 * HALO]

        x_loaded = sem("x_loaded")
        const_loaded = sem("const_loaded")
        taps_loaded = sem("taps_loaded")
        kan_loaded = sem("kan_loaded")
        kan_chunk = sem("kan_chunk")
        pool_step = sem("pool_step")
        halo_loaded = [sem("halo_loaded0"), sem("halo_loaded1")]
        w_clear = sem("w_clear")
        hs_clear = sem("hs_clear")
        f_clear = sem("f_clear")
        sel_ready = sem("sel_ready")
        pool_const = sem("pool_const")
        bias_rep = sem("bias_rep")
        bias_done = sem("bias_done")
        bias_ready = sem("bias_ready")
        mv_ready = sem("mv_ready")
        group_ready = sem("group_ready")
        nv_ready = sem("nv_ready")
        norm_ready = sem("norm_ready")
        xn_ready = sem("xn_ready")
        dve_step = sem("dve_step")
        act_step = sem("act_step")
        hi_ready = sem("hi_ready")
        lo_ready = sem("lo_ready")
        out_done = sem("out_done")
        evac_done = sem("evac_done")
        tile_used = sem("tile_used")
        added = sem("added")
        pool_norm = sem("pool_norm")
        taps_ready = sem("taps_ready")
        turned = sem("turned")
        turned_hi = sem("turned_hi")
        turned_lo = sem("turned_lo")
        chunk_hi = sem("chunk_hi")
        chunk_lo = sem("chunk_lo")
        w_hi = sem("w_hi")
        w_lo = sem("w_lo")
        basis_u = sem("basis_u")
        basis_a = sem("basis_a")
        basis_b = sem("basis_b")
        basis_b3 = sem("basis_b3")
        feat_ready = sem("feat_ready")
        passed = {name: sem("passed_" + name) for name in ("sp", "pe", "dve", "pool")}
        scratch_clear = sem("scratch_clear")
        out_staged = sem("out_staged")
        stored = sem("stored")

        block = ctx.enter_context(nc.Block())
        XV = X[:, :, :].rearrange("p b (y x) -> p b y x", x=WD)
        SV = S[:, :, :, :].rearrange("p s b (y x) -> p s b y x", x=WD)

        def ximg(b):
            return X[:, bass.ds(b, 1), :].rearrange("p a (y x) -> p (a y) x", x=WD)

        def ximg_flat(b):
            return X[:, bass.ds(b, 1), :].rearrange("p a n -> p (a n)")

        def out_bank(outs, o, b):
            return OUT_BANK[o] if len(outs) > 1 else OUT_BANK[b % 2]

        def flat2(a):
            return a.rearrange("p y w -> p (y w)")

        def pass_wait(eng, counter):
            eng.sem_inc(counter, 1)

        def at_half(h, per, n):
            return n if h is None else h * per + n

        ENTRIES = [(par, t) for par in range(2) for t in range(FEATS + 3)]
        ENTRIES_PER_PAIR = len(ENTRIES)
        BASES_PER_PAIR = 2 * (BASES + 3)
        PER = FEATS + 3

        def basis_parts(t):
            return P if t < BASES else (0, 3 * HALO, 3 * HALO, 2 * HALO)[t - BASES]

        LINKS_PER_IMAGE = 5
        PAIR_LINKS = 2 * (3 * (BASES + 3) + 2) + 2 * LINKS_PER_IMAGE
        TILES_OF = {1: 2, 2: PER, 3: 2}

        def tap_columns(kind, n_in):
            return {"cell": n_in * K3 * NG * C, "kan": FEATS * K3 * C, "single": K3 * C}[kind]

        CELL_COLUMNS = [tap_columns("cell", len(ins)) for _, ins, _ in cells]

        def chunk_source(bank, row, columns):
            rows, n = (P, columns) if row < YI else (3 * HALO, min(columns, K3 * NG * C))
            return bank[0:rows, 0:n].rearrange("p (t c) -> p t c", c=C)

        def chunk_dest(part, parity, row, n_tiles, out_row):
            rows, base = (P, 0) if row < YI else (3 * HALO, MAIN_TILES)
            return W[0:rows, parity, part, base:base + n_tiles, out_row * C:(out_row + 1) * C]

        @block.sync
        def _(sp):
            xv = x.rearrange("b c (yb yi) w -> b yi c yb w", yi=YI)
            for b in range(B):
                for yi in range(0, YI, 2):
                    sp.dma_start(XV[C * yi:C * (yi + 1), b], xv[b, yi]).then_inc(x_loaded, 16)
            sp.dma_start(G[:, :], consts[:, 0:P]).then_inc(const_loaded, 16)
            sp.dma_start(IDF[:, :], consts[0:NG * C, P:P + NG * C]).then_inc(const_loaded, 16)
            sp.dma_start(CB[:, :], consts[:, P + NG * C:P + NG * C + 16]).then_inc(const_loaded, 16)
            sp.dma_start(BN_IN[:, :], l0b.rearrange("a r (g c) -> (a r g) c", c=C)).then_inc(const_loaded, 16)
            sp.dma_start(OB_IN[0:1, :], l2bias.rearrange("(a c) -> a c", a=1)).then_inc(const_loaded, 16)
            sp.dma_start(OB_IN[1:2, :], l3bias.rearrange("(a c) -> a c", a=1)).then_inc(const_loaded, 16)
            sp.dma_start(SEL_IN, consts[0:KC, P + NG * C + 16:]).then_inc(const_loaded, 16)

            def wait_both(sem_a, a, sem_b, b):
                sp.wait_ge(sem_a, a)
                pass_wait(sp, passed["sp"])
                sp.wait_ge(sem_b, b)
                pass_wait(sp, passed["sp"])

            def load_taps(k):
                sp.dma_start(RAW[:, :], l0w[k // 4, k % 4].rearrange("o i k d -> o (i k d)"))\
                  .then_inc(taps_loaded, 16)

            sp.wait_ge(hs_clear, 1)
            load_taps(0)
            with sp.Fori(0, HALVES) as h:
                for k in (1, 2):
                    sp.wait_ge(taps_ready, h * NC + k)
                    pass_wait(sp, passed["sp"])
                    load_taps(k)
                for k, (_, ins, outs) in enumerate(cells):
                    for b in range(NB):
                        par = b % 2
                        if k == 0:
                            written, n = xn_ready, h * NB + (b + 1)
                        else:
                            written, n = evac_done, h * OH + (outs_before[k - 1] + (b + 1) * len(cells[k - 1][2]))
                        if b >= 2:
                            wait_both(written, n, lo_ready, h * TH + (tiles_before[k] + (b - 1) * (len(ins) + 1)))
                        elif k:
                            before = tiles_before[k] - (1 - b) * (len(cells[k - 1][1]) + 1)
                            wait_both(written, n, lo_ready, h * TH + before)
                        else:
                            sp.wait_ge(written, n)
                        for g, s in enumerate(ins):
                            at = HALO * g
                            sp.dma_start(HS[at:at + C, par, 1:YB, 1:WD + 1],
                                         SV[P - C:P, s, b, 0:YB - 1, :]).then_inc(halo_loaded[par], 16)
                            sp.dma_start(HS[at + C:at + HALO, par, 0:YB - 1, 1:WD + 1],
                                         SV[0:C, s, b, 1:YB, :]).then_inc(halo_loaded[par], 16)
                        if b == 0 and k + 3 < NC:
                            sp.wait_ge(taps_ready, h * NC + (k + 3))
                            pass_wait(sp, passed["sp"])
                            load_taps(k + 3)
                sp.wait_ge(taps_ready, h * NC + NC)
                pass_wait(sp, passed["sp"])
                load_taps(0)
            sp.wait_ge(taps_loaded, (FILL_AT[0] + 1) * 16)
            sp.dma_start(RAW[0:C, 0:C * 9], l1w.rearrange("o i k d -> o (i k d)")).then_inc(taps_loaded, 16)
            sp.wait_ge(taps_ready, HALVES * NC + 1)
            sp.dma_start(RAW[0:C, 0:C * 9], l3w).then_inc(taps_loaded, 16)

            def halo_block(blk, par):
                src = NS1[par] if blk == 1 else NS[par]
                dst = H1[par] if blk == 1 else HS[:, par]
                for g in range(3 if blk == 2 else 1):
                    top, bot = HALO * g, HALO * g + C
                    sp.dma_start(dst[top:top + C, 1:YB], src[P - C:P, 0:YB - 1])\
                      .then_inc(halo_loaded[par], 16)
                    sp.dma_start(dst[bot:bot + C, 0:YB - 1], src[0:C, 1:YB])\
                      .then_inc(halo_loaded[par], 16)
                if blk == 1:
                    sp.dma_start(dst[0:C, 0:1], src[P - C:P, YB - 1:YB]).then_inc(halo_loaded[par], 16)
                    sp.dma_start(dst[C:HALO, YB - 1:YB], src[0:C, 0:1]).then_inc(halo_loaded[par], 16)

            ov = out.rearrange("b c (yb yi) w -> b yi c yb w", yi=YI)

            for blk in (1, 2):
                n = TILES_OF[blk]
                before = TILES_OF.get(blk - 1, 2)
                for b in range(2):
                    sp.wait_ge(xn_ready, blk * B + (b + 1))
                    sp.wait_ge(lo_ready, T_AT[blk - 1] - (1 - b) * before)
                    halo_block(blk, b)
                with sp.Fori(1, B // 2) as i:
                    for par in range(2):
                        wait_both(xn_ready, i * 2 + (blk * B + par + 1),
                                  lo_ready, i * (2 * n) + (T_AT[blk - 1] + (par - 1) * n))
                        halo_block(blk, par)

            for b in range(B + 2):
                if b < B:
                    sp.wait_ge(xn_ready, 3 * B + b + 1)
                    sp.wait_ge(lo_ready, T_AT[2] + (b - 1) * 2 if b > 1 else T_AT[2] - (1 - b) * PER)
                    halo_block(3, b % 2)
                if b >= 2:
                    sp.wait_ge(out_staged, b - 1)
                    for yi in range(YI):
                        sp.dma_start(ov[b - 2, yi], XV[C * yi:C * (yi + 1), b - 2]).then_inc(stored, 16)
            sp.wait_ge(stored, B * YI * 16)

        @block.gpsimd
        def _(pool):
            pool.memset(NHALF[:, :], -0.5).then_inc(pool_const, 1)
            for par in range(2):
                for part in range(2):
                    last = pool.memset(W[0:3 * HALO, par, part, MAIN_TILES:TILES, :].bitcast(F32), 0.0)
            last.then_inc(w_clear, 1)
            pool.wait_ge(pool_const, 1)

            def norm(cols, images, n):
                pool.wait_ge(nv_ready, n)
                pass_wait(pool, passed["pool"])
                pool.tensor_tensor(RS[:, images], VE[:, cols], NHALF[:, cols], ALU.pow).then_inc(pool_norm, 1)
                pool.wait_ge(pool_norm, n)
                pass_wait(pool, passed["pool"])
                pool.tensor_tensor(NBI[:, images], GM[:, cols, 0], RS[:, images], ALU.mult).then_inc(norm_ready, 1)

            norm(slice(0, B), slice(0, B), 1)

            def rearrange_taps(kind, n):
                pool.wait_ge(taps_loaded, n)
                pass_wait(pool, passed["pool"])
                if kind == "cell":
                    dst = RAWR[:, :, :].rearrange("o (g d) (k c) -> o g d k c", g=NG, c=C)
                    src = RAW[:, :].rearrange("o (g c k d) -> o g d k c", g=NG, c=C, k=K3)
                    for g in range(NG):
                        last = pool.tensor_copy(dst[:, g], src[:, g])
                elif kind == "circular":
                    dst = RAWR[0:C, 0:K3].rearrange("o d (k c) -> o d k c", c=C)
                    src = RAW[0:C, 0:C * 9].rearrange("o (c k d) -> o d k c", c=C, k=K3)
                    for dx in range(K3):
                        for ky in range(K3):
                            last = pool.tensor_copy(dst[:, dx, ky], src[:, K3 - 1 - dx, K3 - 1 - ky])
                else:
                    dst = RAWR[0:C, 0:K3].rearrange("o d (k c) -> o d k c", c=C)
                    last = pool.tensor_copy(dst, RAW[0:C, 0:C * 9].rearrange("o (k d c) -> o d k c", k=K3, c=C))
                last.then_inc(taps_ready, 1)

            o0 = 3 * NB * PIX
            o1 = o0 + NJ * 81 * BASES
            o2 = o1 + NJ * 81
            SPL = flat[0:C, o0:o1].rearrange("o (j a n s) -> o j a n s", j=NJ, a=9, n=9)
            SPF = flat[0:C, o0:o1].rearrange("o (q s) -> o q s", s=BASES)
            SCL = flat[0:C, o1:o2]
            BAS = flat[0:C, o2:o2 + NJ * 81]
            BAV = BAS.rearrange("o (j a n) -> o j a n", j=NJ, a=9)
            SUM = SPF.rearrange("o (j a n) s -> o j a (n s)", j=NJ, a=9)

            def kan_taps(c):
                js = slice(c * NJ, (c + 1) * NJ)
                steps = 17 * c
                pool.dma_start(flat[0:C, o0:o1],
                               l2spline[:, js].rearrange("o j a n s -> o (j a n s)")).then_inc(kan_loaded, 16)
                pool.dma_start(SCL, l2scale[:, js].rearrange("o j a n -> o (j a n)")).then_inc(kan_loaded, 16)
                pool.dma_start(BAS, l2base[:, js].rearrange("o j a n -> o (j a n)")).then_inc(kan_loaded, 16)
                pool.wait_ge(kan_loaded, 48 * (c + 1))
                scl = SCL.rearrange("o (q s) -> o q s", s=1).broadcast_to([C, NJ * 81, BASES])
                pool.tensor_tensor(SPF, SPF, scl, ALU.mult).then_inc(pool_step, 1)
                steps += 1
                for a in range(1, 9):
                    pool.wait_ge(pool_step, steps)
                    pool.tensor_tensor(SUM[:, :, 0], SUM[:, :, 0], SUM[:, :, a], ALU.add).then_inc(pool_step, 1)
                    pool.tensor_tensor(BAV[:, :, 0], BAV[:, :, 0], BAV[:, :, a], ALU.add).then_inc(pool_step, 1)
                    steps += 2
                pool.wait_ge(pool_step, steps)
                kan = KAN[:, :, :].rearrange("o (s d) (k j) -> o d j k s", d=K3, k=K3)[:, :, js]
                spl = SPL[:, :, 0].rearrange("o j (k d) s -> o d j k s", k=K3)
                bas = BAV[:, :, 0].rearrange("o j (k d) -> o d j k", k=K3)
                for dx in range(K3):
                    last = pool.tensor_scalar(kan[:, dx, :, :, 0:BASES], spl[:, dx], -1.0 / 6.0, None, ALU.mult)
                last.then_inc(kan_chunk, 1)
                for dx in range(K3):
                    last = pool.tensor_copy(kan[:, dx, :, :, BASES], bas[:, dx])
                last.then_inc(kan_chunk, 1)
                pool.wait_ge(kan_chunk, 2 * (c + 1))

            kan_chunks = {2: range(0, 2), 3: range(2, 5), 4: range(5, C // NJ)}
            for first in (True, False):
                with (ExitStack() if first else pool.Fori(1, HALVES)) as h:
                    h = 0 if first else h
                    for k in range(NC):
                        if k:
                            pool.wait_ge(turned, h * NC + k)
                            pass_wait(pool, passed["pool"])
                        rearrange_taps("cell", h * (NC * 16) + (k + 1) * 16)
                        if first:
                            for c in kan_chunks.get(k, ()):
                                kan_taps(c)
                    for b in range(NB):
                        norm(slice(b % 2, b % 2 + 1), bass.ds(h * NB + b, 1), h * NB + (b + 2))
            pool.wait_ge(turned, FILL_AT[0])
            rearrange_taps("circular", (HALVES * NC + 2) * 16)
            pool.wait_ge(turned, FILL_AT[1])
            rearrange_taps("conv", (HALVES * NC + 3) * 16)
            with pool.Fori(0, B // 2) as i:
                for par in range(2):
                    norm(slice(par, par + 1), bass.ds(i * 2 + par, 1), i * 2 + (2 + par + B))
            nb = 0
            for first in (True, False):
                with (ExitStack() if first else pool.Fori(1, B // 2)) as i:
                    i = 0 if first else i
                    k = 0
                    for e, (par, t) in enumerate(ENTRIES):
                        if e == 11 and not first:
                            norm(slice(1, 2), bass.ds(i * 2 - 1, 1), i * 2 + (2 + 2 * B - 1))
                        if e == 23:
                            norm(slice(0, 1), bass.ds(i * 2, 1), i * 2 + (2 + 2 * B))
                        if t == BASES:
                            continue
                        k += 1
                        pt = basis_parts(t)
                        pool.wait_ge(basis_b, i * BASES_PER_PAIR + k)
                        pool.tensor_tensor(TB[e % 3][0:pt], TB[e % 3][0:pt], B2[e % 3][0:pt], ALU.mult)\
                            .then_inc(basis_b3, 1)
            norm(slice(1, 2), slice(B - 1, B), 2 + 3 * B - 1)

        def basis_act(act, normalise):
            for first in (True, False):
                with (ExitStack() if first else act.Fori(1, B // 2)) as i:
                    i = 0 if first else i
                    if first:
                        act.wait_ge(out_done, O_AT[3])
                    for par in range(2):
                        b = i * 2 + par
                        normalise(NS[par][:, :, 1:WD + 1], b, b + (2 + B)).then_inc(xn_ready, 1)
                    act.wait_ge(xn_ready, i * 2 + (2 * B + 2))
                    base_u = i * ENTRIES_PER_PAIR
                    nb = 0
                    for e in range(ENTRIES_PER_PAIR + 2):
                        if e < ENTRIES_PER_PAIR:
                            par, t = ENTRIES[e]
                            src, parts = NS[par], P
                            if t > BASES:
                                src, parts = HS[:, par], 3 * HALO
                            if t == BASES + 1:
                                act.wait_ge(halo_loaded[par], i * 96 + (H_AT[1] + 96))
                            if e >= 3:
                                act.wait_ge(feat_ready, base_u + (e - 2))
                            elif not first:
                                act.wait_ge(feat_ready, base_u)
                            u, tb, b2 = UA[e % 3], TB[e % 3], B2[e % 3]
                            pt = basis_parts(t)
                            if pt:
                                col = t if t < BASES else t - 1
                                last = act.activation(u[0:pt], src[0:pt], ACT.Abs, scale=2.5,
                                                      bias=CB[0:pt, col:col + 1])
                            if pt < parts:
                                last = act.activation(u[pt:parts], src[pt:parts], ACT.Tanh, scale=0.5)
                            last.then_inc(basis_u, 1)
                            if pt:
                                nb += 1
                                act.wait_ge(basis_u, base_u + (e + 1))
                                act.activation(tb[0:pt], u[0:pt], ACT.Relu, scale=-1.0, bias=1.0)\
                                   .then_inc(act_step, 1)
                                act.wait_ge(act_step, i * BASES_PER_PAIR + nb)
                                act.activation(b2[0:pt], tb[0:pt], ACT.Square).then_inc(basis_b, 1)
                        if e >= 2:
                            q = e - 2
                            par, t = ENTRIES[q]
                            parts = P if t <= BASES else 3 * HALO
                            if not (first and q < FSLOTS):
                                act.wait_ge(tile_used, base_u + (q + 1 - FSLOTS))
                            act.wait_ge(feat_ready, base_u + (q + 1))
                            act.activation(F[0:parts, q % FSLOTS, 0], FT[q % 3][0:parts], ACT.Copy)\
                               .then_inc(hi_ready, 1)

        @block.scalar
        def _(act):
            xv = x.rearrange("b c (yb yi) w -> b yi c yb w", yi=YI)
            for b in range(B):
                for yi in range(1, YI, 2):
                    act.dma_start(XV[C * yi:C * (yi + 1), b], xv[b, yi]).then_inc(x_loaded, 16)
            act.wait_ge(const_loaded, 112)
            act.activation(SEL[:, :], SEL_IN, ACT.Copy).then_inc(sel_ready, 1)

            def turned_hi_part(columns, n):
                act.wait_ge(turned, n)
                act.activation(WT[:, 0, 0:columns], TR_BANK[0:KC, 0:columns], ACT.Copy).then_inc(turned_hi, 1)

            def banded(kind, n_in, parity, h, at):
                columns = tap_columns(kind, n_in)
                for row in range(CHUNKS):
                    act.wait_ge(chunk_hi, at_half(h, CH, at + row + 1))
                    src = chunk_source(BUILD_HI[(at + row) % 2], row, columns)
                    n = src.shape[1]
                    if row < YI:
                        act.activation(chunk_dest(0, parity, row, n, row), src, ACT.Copy).then_inc(w_hi, 1)
                    else:
                        act.activation(chunk_dest(0, parity, row, n, 0), src, ACT.Copy, scale=MASK[0:3 * HALO, 0:1])
                        act.activation(chunk_dest(0, parity, row, n, YI - 1), src, ACT.Copy,
                                       scale=MASK[0:3 * HALO, 1:2]).then_inc(w_hi, 1)

            def normalise(dst, b, n):
                act.wait_ge(norm_ready, n)
                return act.activation(dst, ximg(b), ACT.Identity, bias=NBI[:, bass.ds(b, 1)],
                                      scale=RS[:, bass.ds(b, 1)])

            def split_hi(h, k, b):
                ins = cells[k][1]
                par = b % 2
                if k == 0:
                    act.wait_ge(xn_ready, h * NB + (b + 1))
                else:
                    act.wait_ge(evac_done, h * OH + (outs_before[k - 1] + (b + 1) * len(cells[k - 1][2])))
                if b >= 2:
                    act.wait_ge(out_done, h * OH + (outs_before[k] + (b - 1) * len(cells[k][2])))
                elif k:
                    act.wait_ge(out_done, h * OH + (outs_before[k] - (1 - b) * len(cells[k - 1][2])))
                for g, s in enumerate(ins):
                    act.activation(F[:, par * 4 + g, 0, :, 1:WD + 1], SV[:, s, b], ACT.Copy)\
                       .then_inc(hi_ready, 1)
                n = len(ins)
                loads = halo_before[k] + (b // 2 + 1) * 2 * n * 16
                act.wait_ge(halo_loaded[par], h * HH + loads)
                act.activation(F[0:HALO * n, par * 4 + n, 0, :, 1:WD + 1],
                               HS[0:HALO * n, par, :, 1:WD + 1], ACT.Copy).then_inc(hi_ready, 1)

            act.wait_ge(f_clear, 1)
            act.wait_ge(w_clear, 1)
            with act.Fori(0, HALVES) as h:
                turned_hi_part(CELL_COLUMNS[0], h * NC + 1)
                for b in range(NB):
                    normalise(SV[:, 0, b], h * NB + b, 1).then_inc(xn_ready, 1)
                banded("cell", len(cells[0][1]), 0, h, 0)
                turned_hi_part(CELL_COLUMNS[1], h * NC + 2)
                split_hi(h, 0, 0)
                for k, (cell, ins, outs) in enumerate(cells):
                    if k + 1 < NC:
                        banded("cell", len(cells[k + 1][1]), (k + 1) % 2, h, chunks_before[k + 1])
                    if k + 2 < NC:
                        turned_hi_part(CELL_COLUMNS[k + 2], h * NC + (k + 3))
                    if k == 3:
                        act.wait_ge(kan_chunk, 2 * (C // NJ))
                    for b in range(NB):
                        if b + 1 < NB:
                            split_hi(h, k, b + 1)
                        elif k + 1 < NC:
                            split_hi(h, k + 1, 0)
                        for o, (group, slot) in enumerate(outs):
                            act.wait_ge(out_done, h * OH + (outs_before[k] + b * len(outs) + o + 1))
                            act.activation(S[:, slot, b], out_bank(outs, o, b)[:, :], ACT.Relu,
                                           bias=BIAS[:, cell * NG + group:cell * NG + group + 1])\
                               .then_inc(evac_done, 1)

            turned_hi_part(K3 * C, FILL_AT[0] + 1)
            banded("single", 1, 0, None, C_AT[0])
            turned_hi_part(FEATS * K3 * C, FILL_AT[1] + 1)
            banded("kan", 1, 1, None, C_AT[1])
            turned_hi_part(K3 * C, FILL_AT[2] + 1)

            def split_block(blk, i, par):
                b = i * 2 + par
                dst = NS1[par] if blk == 1 else NS[par]
                n = b + (2 + (blk - 1) * B)
                last = normalise(dst[:, :, 1:WD + 1], b, n)
                if blk == 1:
                    for col, src in ((0, WD - 1), (WD + 1, 0)):
                        last = act.activation(dst[:, :, col:col + 1], ximg(b)[:, :, src:src + 1], ACT.Identity,
                                              bias=NBI[:, bass.ds(b, 1)], scale=RS[:, bass.ds(b, 1)])
                last.then_inc(xn_ready, 1)
                act.wait_ge(xn_ready, b + (blk * B + 1))
                act.activation(F[:, par * 4, 0], dst, ACT.Copy).then_inc(hi_ready, 1)
                halo = H1[par] if blk == 1 else HS[:, par]
                per = (4 if blk == 1 else 2) * 16
                act.wait_ge(halo_loaded[par], i * per + (H_AT[blk - 1] + per))
                act.activation(F[0:HALO, par * 4 + 1, 0], halo[0:HALO], ACT.Copy).then_inc(hi_ready, 1)

            act.wait_ge(scratch_clear, 1)
            for blk in (1, 2, 3):
                if blk == 2:
                    banded("single", 1, 0, None, C_AT[2])
                    basis_act(act, normalise)
                    continue
                for b in range(2):
                    if blk == 1:
                        act.wait_ge(out_done, O_AT[1])
                    else:
                        act.wait_ge(tile_used, PER * B)
                    split_block(blk, 0, b)
                with act.Fori(1, B // 2) as i:
                    for par in range(2):
                        act.wait_ge(out_done, i * 2 + (O_AT[blk] + par - 1))
                        split_block(blk, i, par)

        @block.vector
        def _(dve):
            steps = Count()

            nc.vector.memset(HS[:, :, :, :], 0.0).then_inc(hs_clear, 1)
            edges = F[:, :, :, :, :].bitcast(F32).rearrange("p s a y w -> p (s a y) w")
            for col in (0, WD + 1):
                last = nc.vector.memset(edges[:, :, col:col + 1], 0.0)
            last.then_inc(f_clear, 1)

            dve.wait_ge(const_loaded, 112)
            for yi in range(YI):
                nc.vector.tensor_copy(BN_REP[:, yi], BN_IN[:, :])
                last = nc.vector.tensor_copy(OB_REP[:, yi], OB_IN[:, :])
            last.then_inc(bias_rep, 1)

            dve.wait_ge(x_loaded, 16 * YI * B)
            for b in range(B):
                last = nc.vector.bn_stats(STATS[:, b], X[:, b])
            last.then_inc(dve_step, 1)
            dve.wait_ge(dve_step, steps.next())
            for b in range(B):
                last = nc.vector.bn_aggr(MV[:, b], STATS[:, b])
            last.then_inc(dve_step, 1)
            dve.wait_ge(dve_step, steps.next())

            def squares(cols):
                m, v = MV[:, cols, 0], MV[:, cols, 1]
                nc.vector.tensor_tensor(NV[:, cols], m, m, ALU.mult).then_inc(dve_step, 1)
                dve.wait_ge(dve_step, steps.next())
                nc.vector.scalar_tensor_tensor(v, v, GN_EPS, NV[:, cols], ALU.add, ALU.add).then_inc(mv_ready, 1)

            def group_stats(cols, bank, n):
                dve.wait_ge(group_ready, n)
                g = GM[:, cols, :].rearrange("p b a -> p (b a)")
                nc.vector.tensor_scalar(g, bank[:, 2 * cols.start:2 * cols.stop], -1.0, None, ALU.mult)\
                    .then_inc(dve_step, 1)
                dve.wait_ge(dve_step, steps.next())
                m, v = GM[:, cols, 0], GM[:, cols, 1]
                nc.vector.tensor_tensor(NV[:, cols], m, m, ALU.mult).then_inc(dve_step, 1)
                dve.wait_ge(dve_step, steps.next())
                nc.vector.scalar_tensor_tensor(VE[:, cols], NV[:, cols], -1.0, v, ALU.mult, ALU.subtract)\
                    .then_inc(nv_ready, 1)

            def image_stats(b, par):
                nc.vector.bn_stats(STATS[:, par], ximg_flat(b)).then_inc(dve_step, 1)
                dve.wait_ge(dve_step, steps.next())
                pass_wait(dve, passed["dve"])
                nc.vector.bn_aggr(MV[:, par], STATS[:, par]).then_inc(dve_step, 1)
                dve.wait_ge(dve_step, steps.next())
                squares(slice(par, par + 1))

            squares(slice(0, B))
            group_stats(slice(0, B), STAT_BANK[0], 1)
            dve.wait_ge(bias_done, 1)
            nc.vector.tensor_copy(BIAS[:, :], OUT_BANK[0][:, 0:NG * C])
            nc.vector.tensor_copy(OB[:, :], OUT_BANK[0][:, 64:66]).then_inc(bias_ready, 1)

            def turned_lo_part(columns, n):
                dve.wait_ge(turned_hi, n)
                nc.vector.tensor_tensor(WT[:, 1, 0:columns], TR_BANK[0:KC, 0:columns],
                                        WT[:, 0, 0:columns].bitcast(F32), ALU.subtract).then_inc(turned_lo, 1)

            def banded(kind, n_in, parity, h, at):
                columns = tap_columns(kind, n_in)
                for row in range(CHUNKS):
                    dve.wait_ge(chunk_lo, at_half(h, CH, at + row + 1))
                    src = chunk_source(BUILD_LO[(at + row) % 2], row, columns)
                    n = src.shape[1]
                    if row < YI:
                        nc.vector.tensor_copy(chunk_dest(1, parity, row, n, row), src).then_inc(w_lo, 1)
                    else:
                        nc.vector.tensor_scalar(chunk_dest(1, parity, row, n, 0), src,
                                                MASK[0:3 * HALO, 0:1], None, ALU.mult)
                        nc.vector.tensor_scalar(chunk_dest(1, parity, row, n, YI - 1), src,
                                                MASK[0:3 * HALO, 1:2], None, ALU.mult).then_inc(w_lo, 1)

            def split_lo(h, k, b):
                ins = cells[k][1]
                par, n = b % 2, len(ins)
                at = tiles_before[k] + b * (n + 1)
                for g, s in enumerate(ins):
                    dve.wait_ge(hi_ready, h * TH + (at + g + 1))
                    nc.vector.tensor_tensor(F[:, par * 4 + g, 1, :, 1:WD + 1], SV[:, s, b],
                                            F[:, par * 4 + g, 0, :, 1:WD + 1].bitcast(F32), ALU.subtract)\
                        .then_inc(lo_ready, 1)
                dve.wait_ge(hi_ready, h * TH + (at + n + 1))
                rows = slice(0, HALO * n)
                nc.vector.tensor_tensor(F[rows, par * 4 + n, 1, :, 1:WD + 1], HS[rows, par, :, 1:WD + 1],
                                        F[rows, par * 4 + n, 0, :, 1:WD + 1].bitcast(F32), ALU.subtract)\
                    .then_inc(lo_ready, 1)

            def tail(b, par, blk):
                dve.wait_ge(norm_ready, b + (1 + blk * B))
                group_stats(slice(par, par + 1), STAT_BANK[par], b + (2 + blk * B))

            half_links = NB * LINKS_PER_IMAGE
            links0 = steps.n + steps.base
            with dve.Fori(0, HALVES) as h:
                steps.enter(h * half_links + links0)
                turned_lo_part(CELL_COLUMNS[0], h * NC + 1)
                banded("cell", len(cells[0][1]), 0, h, 0)
                turned_lo_part(CELL_COLUMNS[1], h * NC + 2)
                split_lo(h, 0, 0)
                for k, (cell, ins, outs) in enumerate(cells):
                    if k + 1 < NC:
                        banded("cell", len(cells[k + 1][1]), (k + 1) % 2, h, chunks_before[k + 1])
                    if k + 2 < NC:
                        turned_lo_part(CELL_COLUMNS[k + 2], h * NC + (k + 3))
                    for b in range(NB):
                        if b + 1 < NB:
                            split_lo(h, k, b + 1)
                        elif k + 1 < NC:
                            split_lo(h, k + 1, 0)
                        if k == NC - 1:
                            img = h * NB + b
                            dve.wait_ge(evac_done, h * OH + (outs_before[k] + b + 1))
                            nc.vector.tensor_tensor(ximg_flat(img), ximg_flat(img), S[:, outs[0][1], b], ALU.add)\
                                .then_inc(added, 1)
                            dve.wait_ge(added, img + 1)
                            pass_wait(dve, passed["dve"])
                            image_stats(img, b % 2)
                            if b:
                                tail(h * NB + (b - 1), (b - 1) % 2, 0)
                tail(h * NB + (NB - 1), (NB - 1) % 2, 0)
                assert steps.n == half_links
            steps.enter(links0 + HALVES * half_links)

            for par in range(2):
                for col in (0, WD + 1):
                    last = nc.vector.memset(NS[par][:, :, col:col + 1], 0.0)
            last.then_inc(scratch_clear, 1)

            turned_lo_part(K3 * C, FILL_AT[0] + 1)
            banded("single", 1, 0, None, C_AT[0])
            turned_lo_part(FEATS * K3 * C, FILL_AT[1] + 1)
            banded("kan", 1, 1, None, C_AT[1])
            turned_lo_part(K3 * C, FILL_AT[2] + 1)

            def split_block(blk, b, par):
                src = NS1[par] if blk == 1 else NS[par]
                halo = H1[par] if blk == 1 else HS[:, par]
                dve.wait_ge(hi_ready, b * 2 + (T_AT[blk - 1] + 1))
                nc.vector.tensor_tensor(F[:, par * 4, 1], src, F[:, par * 4, 0].bitcast(F32), ALU.subtract)\
                    .then_inc(lo_ready, 1)
                dve.wait_ge(hi_ready, b * 2 + (T_AT[blk - 1] + 2))
                nc.vector.tensor_tensor(F[0:HALO, par * 4 + 1, 1], halo[0:HALO],
                                        F[0:HALO, par * 4 + 1, 0].bitcast(F32), ALU.subtract)\
                    .then_inc(lo_ready, 1)

            def update(blk, b, par):
                if blk == 2:
                    dve.wait_ge(tile_used, b * PER + PER)
                else:
                    dve.wait_ge(out_done, b + (O_AT[blk] + 1))
                psum, ximage = OUT_BANK[par][:, :], ximg_flat(b)
                if blk == 1:
                    nc.vector.tensor_tensor(ximage, psum, ximage, ALU.add).then_inc(added, 1)
                elif blk == 2:
                    nc.vector.scalar_tensor_tensor(ximage, psum, OB[:, 0:1], ximage, ALU.add, ALU.add)\
                        .then_inc(added, 1)
                else:
                    nc.vector.scalar_tensor_tensor(ximage, psum, OB[:, 1:2], ximage, ALU.add, ALU.add)\
                        .then_inc(out_staged, 1)
                if blk < 3:
                    dve.wait_ge(added, b + (blk * B + 1))
                    pass_wait(dve, passed["dve"])
                    image_stats(b, par)

            split_block(1, 0, 0)
            split_block(1, 1, 1)
            update(1, 0, 0)
            links1 = steps.n + steps.base
            with dve.Fori(1, B // 2) as i:
                steps.enter((i - 1) * (2 * LINKS_PER_IMAGE) + links1)
                for par in range(2):
                    split_block(1, i * 2 + par, par)
                    update(1, i * 2 + (par - 1), 1 - par)
                    tail(i * 2 + (par - 2), par, 1)
                assert steps.n == 2 * LINKS_PER_IMAGE
            steps.enter(links1 + (B // 2 - 1) * 2 * LINKS_PER_IMAGE)
            update(1, B - 1, 1)
            tail(B - 2, 0, 1)
            tail(B - 1, 1, 1)

            banded("single", 1, 0, None, C_AT[2])

            for first in (True, False):
                if not first:
                    links2 = steps.n + steps.base
                with (ExitStack() if first else dve.Fori(1, B // 2)) as i:
                    if first:
                        i = 0
                    else:
                        steps.enter((i - 1) * PAIR_LINKS + links2)
                    base_u = i * ENTRIES_PER_PAIR
                    base_b = i * BASES_PER_PAIR
                    nb = 0
                    counts = {}
                    for e in range(ENTRIES_PER_PAIR + 3):
                        if e < ENTRIES_PER_PAIR:
                            par, t = ENTRIES[e]
                            pt = basis_parts(t)
                            parts = P if t <= BASES else 3 * HALO
                            u, a, a2 = UA[e % 3], TA[e % 3], A2[e % 2]
                            dve.wait_ge(basis_u, base_u + (e + 1))
                            if pt:
                                nb += 1
                                counts[e] = nb
                                nc.vector.tensor_scalar(a[0:pt], u[0:pt], 2.0, 2.0, ALU.min, ALU.subtract)\
                                    .then_inc(dve_step, 1)
                                dve.wait_ge(dve_step, steps.next())
                                nc.vector.tensor_tensor(a2[0:pt], a[0:pt], a[0:pt], ALU.mult).then_inc(dve_step, 1)
                                dve.wait_ge(dve_step, steps.next())
                                nc.vector.tensor_tensor(a2[0:pt], a2[0:pt], a[0:pt], ALU.mult).then_inc(dve_step, 1)
                                dve.wait_ge(dve_step, steps.next())
                            if pt < parts:
                                nc.vector.tensor_scalar(a[pt:parts], u[pt:parts], 0.5, 0.5, ALU.mult, ALU.add)\
                                    .then_inc(dve_step, 1)
                                dve.wait_ge(dve_step, steps.next())
                        if 1 <= e <= ENTRIES_PER_PAIR:
                            q = e - 1
                            par, t = ENTRIES[q]
                            pt = basis_parts(t)
                            parts = P if t <= BASES else 3 * HALO
                            src = NS[par] if t <= BASES else HS[:, par]
                            if pt < parts:
                                last = nc.vector.tensor_tensor(FT[q % 3][pt:parts], TA[q % 3][pt:parts],
                                                               src[pt:parts], ALU.mult)
                            if pt:
                                dve.wait_ge(basis_b3, base_b + counts[q])
                                last = nc.vector.scalar_tensor_tensor(
                                    flat2(FT[q % 3])[0:pt], flat2(TB[q % 3])[0:pt], 4.0,
                                    flat2(A2[q % 2])[0:pt], ALU.mult, ALU.add)
                            last.then_inc(feat_ready, 1)
                        if e >= 3:
                            q = e - 3
                            par, t = ENTRIES[q]
                            parts = P if t <= BASES else 3 * HALO
                            dve.wait_ge(feat_ready, base_u + (q + 1))
                            dve.wait_ge(hi_ready, base_u + (T_AT[1] + q + 1))
                            nc.vector.tensor_tensor(F[0:parts, q % FSLOTS, 1], FT[q % 3][0:parts],
                                                    F[0:parts, q % FSLOTS, 0].bitcast(F32), ALU.subtract)\
                                .then_inc(lo_ready, 1)
                        if e == 5 and not first:
                            update(2, i * 2 - 1, 1)
                        if e == 11 and not first:
                            tail(i * 2 - 1, 1, 2)
                        if e == 17:
                            update(2, i * 2, 0)
                        if e == 23:
                            tail(i * 2, 0, 2)
                    if not first:
                        assert steps.n == PAIR_LINKS
            steps.enter(links2 + (B // 2 - 1) * PAIR_LINKS)
            update(2, B - 1, 1)
            tail(B - 1, 1, 2)

            split_block(3, 0, 0)
            split_block(3, 1, 1)
            update(3, 0, 0)
            with dve.Fori(1, B // 2) as i:
                for par in range(2):
                    split_block(3, i * 2 + par, par)
                    update(3, i * 2 + (par - 1), 1 - par)
            update(3, B - 1, 1)

        @block.tensor
        def _(pe):
            pe.wait_ge(const_loaded, 112)
            pe.wait_ge(bias_rep, 1)
            nc.tensor.matmul(OUT_BANK[0][:, 0:NG * C], BN_REP[:, :, :].rearrange("k y c -> k (y c)"), IDF[:, :],
                             start=True, stop=True)
            nc.tensor.matmul(OUT_BANK[0][:, 64:66], OB_REP[:, :, :].rearrange("k y c -> k (y c)"), IDF[0:2, 0:2],
                             start=True, stop=True).then_inc(bias_done, 1)
            pe.wait_ge(mv_ready, 1)
            nc.tensor.matmul(STAT_BANK[0][:, 0:2 * B], G[:, :], MV[:, :, :].rearrange("p b a -> p (b a)"),
                             start=True, stop=True).then_inc(group_ready, 1)

            def group_means(par, n):
                pe.wait_ge(mv_ready, n)
                nc.tensor.matmul(STAT_BANK[par][:, 2 * par:2 * par + 2], G[:, :], MV[:, par, :],
                                 start=True, stop=True).then_inc(group_ready, 1)

            def turn_taps(kind, n_in, n_ready):
                if kind == "kan":
                    pe.wait_ge(kan_chunk, n_ready)
                else:
                    pe.wait_ge(taps_ready, n_ready)
                    pass_wait(pe, passed["pe"])
                co = NG * C if kind == "cell" else C
                src = KAN if kind == "kan" else RAWR
                for q in range(tap_columns(kind, n_in) // co):
                    last = nc.tensor.matmul(TR_BANK[0:KC, q * co:(q + 1) * co], src[0:co, q, :], IDF[0:co, 0:co],
                                            start=True, stop=True)
                last.then_inc(turned, 1)

            def halo_taps(kind, part, g):
                if kind == "kan":
                    return WT[:, part, :].rearrange("k (t g n) -> k g t n", t=K3, g=K3)[:, g]
                n = K3 * NG * C if kind == "cell" else K3 * C
                return WT[:, part, g * n:(g + 1) * n]

            def build_banded(kind, n_in, h, at, n_turned):
                pe.wait_ge(turned_hi, n_turned)
                pe.wait_ge(turned_lo, n_turned)
                columns = tap_columns(kind, n_in)
                for row in range(CHUNKS):
                    cc = at + row
                    for part, banks, free, built in ((0, BUILD_HI, w_hi, chunk_hi), (1, BUILD_LO, w_lo, chunk_lo)):
                        if h is None or cc >= 2:
                            pe.wait_ge(free, at_half(h, CH, cc - 1))
                        bank = banks[cc % 2]
                        if row < YI:
                            last = nc.tensor.matmul(bank[:, 0:columns], SEL[:, row * P:(row + 1) * P],
                                                    WT[:, part, 0:columns], start=True, stop=True)
                        else:
                            groups = {"cell": n_in, "kan": NG, "single": 1}[kind]
                            for g in range(groups):
                                taps = halo_taps(kind, part, g)
                                s = YI * P + g * 3 * HALO
                                n = min(columns, K3 * NG * C)
                                last = nc.tensor.matmul(bank[0:3 * HALO, 0:n], SEL[:, s:s + 3 * HALO], taps,
                                                        start=g == 0, stop=g == groups - 1)
                        last.then_inc(built, 1)

            PRODUCTS = ((0, 0), (0, 1), (1, 0))

            def convolve(bank, parity, terms, open_, close):
                todo = [(tile + dx * step, slot, rows, dx, wp, fp) for tile, step, slot, rows in terms
                        for dx in range(K3) for wp, fp in PRODUCTS]
                for n, (tile, slot, rows, dx, wp, fp) in enumerate(todo):
                    last = nc.tensor.matmul(bank[:, :].rearrange("p (y x) -> p y x", x=WD),
                                            W[0:rows, parity, wp, tile, :], F[0:rows, slot, fp, :, dx:dx + WD],
                                            start=open_ and n == 0, stop=close and n == len(todo) - 1)
                return last

            def cell_step(h, k, b, par):
                _, ins, outs = cells[k]
                n, m = len(ins), len(outs)
                if par == 0:
                    pe.wait_ge(w_hi, h * CH + chunks_before[k + 1])
                    pe.wait_ge(w_lo, h * CH + chunks_before[k + 1])
                    if k:
                        pe.wait_ge(evac_done, h * OH + outs_before[k])
                at = b * (n + 1) + (tiles_before[k] + n + 1)
                pe.wait_ge(hi_ready, h * TH + at)
                pe.wait_ge(lo_ready, h * TH + at)
                for o, (group, _) in enumerate(outs):
                    if m > 1:
                        if not (k == 0 and isinstance(b, int) and b == 0):
                            pe.wait_ge(evac_done, h * OH + (b * m + (outs_before[k] - m + o + 1)))
                    elif not (k == 0 and isinstance(b, int) and b < 2):
                        pe.wait_ge(evac_done, h * OH + (b + (outs_before[k] - 1)))
                    terms = [(g * K3 * NG + group, NG, par * 4 + g, P) for g in range(n)]
                    terms.append((MAIN_TILES + group, NG, par * 4 + n, HALO * n))
                    convolve(out_bank(outs, o, par), k % 2, terms, True, True).then_inc(out_done, 1)

            pe.wait_ge(sel_ready, 1)
            pe.wait_ge(bias_ready, 1)
            with pe.Fori(0, HALVES) as h:
                pe.wait_ge(nv_ready, h * NB + 1)
                turn_taps("cell", len(cells[0][1]), h * NC + 1)
                build_banded("cell", len(cells[0][1]), h, 0, h * NC + 1)
                turn_taps("cell", len(cells[1][1]), h * NC + 2)
                for k, (_, ins, outs) in enumerate(cells):
                    if k + 1 < NC:
                        build_banded("cell", len(cells[k + 1][1]), h, chunks_before[k + 1], h * NC + (k + 2))
                    if k + 2 < NC:
                        turn_taps("cell", len(cells[k + 2][1]), h * NC + (k + 3))
                    if k == 0:
                        for b in range(NB):
                            cell_step(h, k, b, b % 2)
                    elif k < NC - 1:
                        with pe.Fori(0, NB // 2) as i:
                            for par in range(2):
                                cell_step(h, k, i * 2 + par, par)
                    else:
                        for b in range(NB):
                            cell_step(h, k, b, b % 2)
                            if b:
                                img = h * NB + (b - 1)
                                group_means((b - 1) % 2, img + 2)
                        img = h * NB + (NB - 1)
                        group_means((NB - 1) % 2, img + 2)

            pe.wait_ge(nv_ready, 1 + B)
            turn_taps("single", 1, HALVES * NC + 1)
            build_banded("single", 1, None, C_AT[0], FILL_AT[0] + 1)
            turn_taps("kan", 1, 2 * (C // NJ))
            build_banded("kan", 1, None, C_AT[1], FILL_AT[1] + 1)
            turn_taps("single", 1, HALVES * NC + 2)

            def block_step(blk, b, par):
                pe.wait_ge(hi_ready, b * 2 + (T_AT[blk - 1] + 2))
                pe.wait_ge(lo_ready, b * 2 + (T_AT[blk - 1] + 2))
                convolve(OUT_BANK[par], 0, [(0, 1, par * 4, P), (MAIN_TILES, 1, par * 4 + 1, HALO)], True, True)\
                    .then_inc(out_done, 1)

            pe.wait_ge(w_hi, C_AT[1])
            pe.wait_ge(w_lo, C_AT[1])
            pe.wait_ge(evac_done, HALVES * OH)
            block_step(1, 0, 0)
            block_step(1, 1, 1)
            pe.wait_ge(turned_hi, FILL_AT[2] + 1)
            pe.wait_ge(turned_lo, FILL_AT[2] + 1)
            group_means(0, 2 + B)
            with pe.Fori(1, B // 2) as i:
                for par in range(2):
                    pe.wait_ge(added, i * 2 + (B + par - 1))
                    block_step(1, i * 2 + par, par)
                    group_means(1 - par, i * 2 + (par - 1 + 2 + B))
            group_means(1, 2 + B + B - 1)
            build_banded("single", 1, None, C_AT[2], FILL_AT[2] + 1)

            pe.wait_ge(w_hi, C_AT[2])
            pe.wait_ge(w_lo, C_AT[2])
            pe.wait_ge(added, 2 * B)
            for first in (True, False):
                with (ExitStack() if first else pe.Fori(1, B // 2)) as i:
                    i = 0 if first else i
                    for e, (par, t) in enumerate(ENTRIES):
                        if t == 0 and not first:
                            pe.wait_ge(added, i * 2 + (2 * B + par - 1))
                        pe.wait_ge(hi_ready, i * ENTRIES_PER_PAIR + (T_AT[1] + e + 1))
                        pe.wait_ge(lo_ready, i * ENTRIES_PER_PAIR + (T_AT[1] + e + 1))
                        if t <= BASES:
                            term = (t * K3, 1, e % FSLOTS, P)
                        else:
                            term = (MAIN_TILES + (t - FEATS) * K3, 1, e % FSLOTS, 3 * HALO)
                        convolve(OUT_BANK[par], 1, [term], t == 0, t == PER - 1).then_inc(tile_used, 1)
                        if e == 7 and not first:
                            group_means(1, i * 2 + (1 + 2 * B))
                        if e == 19:
                            group_means(0, i * 2 + (2 + 2 * B))
            group_means(1, 1 + 3 * B)

            pe.wait_ge(w_hi, C_AT[2] + CHUNKS)
            pe.wait_ge(w_lo, C_AT[2] + CHUNKS)
            pe.wait_ge(added, 3 * B)
            block_step(3, 0, 0)
            block_step(3, 1, 1)
            with pe.Fori(1, B // 2) as i:
                for par in range(2):
                    pe.wait_ge(out_staged, i * 2 + (par - 1))
                    block_step(3, i * 2 + par, par)


_INS = ["x", "L0_conv_W", "L0_conv_b", "L1_conv_weight", "L2_conv_base_weight", "L2_conv_spline_weight",
        "L2_conv_spline_scaler", "L2_conv_bias_weight", "L3_conv_combinator", "L3_conv_bias"]


def shape_constants():
    n_sel = YI * P + NG * 3 * HALO
    c = np.zeros((P, P + NG * C + 16 + n_sel), np.float32)
    ch = np.arange(P) % C
    c[:, 0:P] = (ch[:, None] // 2 == ch[None, :] // 2) / 16.0
    c[0:NG * C, P:P + NG * C] = np.eye(NG * C)
    at = P + NG * C
    for i in range(BASES):
        c[:, at + i] = 3.5 - i
    for t in range(3):
        c[:, at + BASES + t] = 3.5 - (3 * t + np.arange(P) // HALO)
    for side in range(2):
        c[:, at + BASES + 3 + side] = np.arange(P) // C % 2 == side
    at += 16
    ky, k_c = np.arange(KC) // C, np.arange(KC) % C
    for j in range(YI):
        c[0:KC, at + j * P:at + (j + 1) * P] = ((np.arange(P) // C == j + ky[:, None] - 1)
                                                & (ch == k_c[:, None]))
    rows = np.arange(3 * HALO)
    for g in range(NG):
        s = at + YI * P + g * 3 * HALO
        c[0:KC, s:s + 3 * HALO] = ((rows // HALO == g) & (ky[:, None] == 2 * (rows // C % 2))
                                   & (rows % C == k_c[:, None]))
    return c


def kernel(**inputs):
    import concourse.bacc as bacc
    from concourse.bass_utils import run_bass_kernel_spmd

    nc = bacc.Bacc("TRN2", target_bir_lowering=False, num_devices=1)
    arrays, args = {}, []
    for name in _INS:
        a = np.ascontiguousarray(inputs[name])
        arrays[f"in_{name}"] = a
        args.append(nc.dram_tensor(f"in_{name}", a.shape, mybir.dt.from_np(a.dtype), kind="ExternalInput").ap())
    consts = shape_constants()
    arrays["in_consts"] = consts
    args.append(nc.dram_tensor("in_consts", consts.shape, mybir.dt.float32, kind="ExternalInput").ap())
    out = nc.dram_tensor("out_0", (B, C, YI * YB, WD), mybir.dt.float32, kind="ExternalOutput").ap()
    build(nc, *args, out)
    r = run_bass_kernel_spmd(nc, [arrays], core_ids=[0])
    return r.results[0]["out_0"]
```

```python
from contextlib import ExitStack

import numpy as np
import concourse.bass as bass
from concourse import mybir

P = 128
C = 16
YI = 8
YB = 8
WD = 64
PW = WD + 2
PIX = YB * WD
B = 8
X_SPLIT = 5
OUT_SPLIT = 5
KAN_AFTER = 1
RING = 4
HALVES = 2
NB = B // HALVES
HALO = 2 * C
K3 = 3
NG = 3
KC = K3 * C
TAP_BLOCKS = 9
TRIPLE = 3
CHUNKS = TRIPLE + 1
MAIN_TILES = NG * K3 * NG
TILES = MAIN_TILES + K3 * NG
FSLOTS = 8
BASES = 8
NJ = 2
FEATS = BASES + 1
CB_COLUMNS = 48
HALO_FEATS = 3
EDGE_TILES = HALO_FEATS
RING2 = 6

RIGHT, UP, DOWN = range(3)
GN_EPS = 1e-5


class Count:

    def __init__(self):
        self.base, self.n = 0, 0

    def next(self):
        self.n += 1
        return self.base + self.n

    def enter(self, base):
        self.base, self.n = base, 0


def lattice():
    cells = []
    for col in range(4):
        for row in range(4):
            if col == 0:
                ins = [0] if row == 0 else [3 + row]
            elif row == 0:
                ins = [0, 4]
            elif row == 3:
                ins = [3, 6]
            else:
                ins = [row, 4 + row, 3 + row]
            outs = []
            if col < 3 or row == 3:
                outs.append((RIGHT, row))
            if row > 0 and col < 3:
                outs.append((UP, 3 + row))
            if row < 3:
                outs.append((DOWN, 4 + row))
            cells.append((col * 4 + row, ins, outs))
    return cells


def halo_tiles(ins):
    return 1 if len(ins) == NG else len(ins)


def halo_dmas(ins):
    return 2 * NG if len(ins) == NG else 2 * K3


def build(nc, x, l0w, l0b, l1w, l2base, l2spline, l2scale, l2bias, l3w, l3bias, consts, out):
    F32, F32R = mybir.dt.float32, mybir.dt.float32r
    ALU, ACT = mybir.AluOpType, mybir.ActivationFunctionType
    cells = lattice()
    NC = len(cells)

    tiles_before, outs_before, chunks_before, halo_before = [0], [0], [0], [0]
    for _, ins, outs in cells:
        tiles_before.append(tiles_before[-1] + NB * (len(ins) + halo_tiles(ins)))
        outs_before.append(outs_before[-1] + NB * len(outs))
        chunks_before.append(chunks_before[-1] + CHUNKS)
        halo_before.append(halo_before[-1] + NB // 2 * halo_dmas(ins) * 16)
    TH, OH, CH, HH = tiles_before[-1], outs_before[-1], chunks_before[-1], halo_before[-1]
    assert CH % 2 == 0
    T_AT = [HALVES * TH, HALVES * TH + 2 * B, HALVES * TH + 2 * B + EDGE_TILES + FEATS * B]
    O_AT = {1: HALVES * OH, 3: HALVES * OH + B}
    C_AT = [HALVES * CH, HALVES * CH + CHUNKS, HALVES * CH + 2 * CHUNKS]
    ORDER = [("rows", 0), ("rows", 1)]
    for b in range(B):
        ORDER += [("halo", b)] + ([("rows", b + 2)] if b + 2 < B else [])
    ORDER_AT = {tile: n + 1 for n, tile in enumerate(ORDER)}
    FILL_AT = [HALVES * NC, HALVES * NC + 1, HALVES * NC + 2]

    ctx = ExitStack()
    with ctx:
        def sb(name, shape, dt=F32):
            return ctx.enter_context(nc.sbuf_tensor(name, shape, dt))

        def sem(name):
            return ctx.enter_context(nc.semaphore(name))

        X = sb("X", [P, B, PIX])
        S = sb("S", [P, 7, NB, YB, PW])
        F = sb("F", [P, FSLOTS, 2, YB, PW], F32R)
        W = sb("W", [P, 2, 2, TILES, P], F32R)
        HS = sb("HS", [3 * HALO, 4, YB, PW])
        RAW = sb("RAW", [NG * C, NG * C * 9])
        RAWR = sb("RAWR", [NG * C, TAP_BLOCKS, KC])
        WT = sb("WT", [KC, 2, TAP_BLOCKS * NG * C], F32R)
        SEL = sb("SEL", [KC, TRIPLE * P + NG * 3 * HALO], F32R)
        RAW_ONE = [sb(f"RAW_ONE{i}", [C, C * 9]) for i in range(2)]
        KAN = sb("KAN", [P, FEATS * K3, KC])
        G = sb("G", [P, P])
        CB = sb("CB", [P, CB_COLUMNS])
        IDF = sb("IDF", [NG * C, NG * C])
        BN_IN = sb("BN_IN", [NG * C, C])
        BN_REP = sb("BN_REP", [NG * C, YI, C])
        BIAS = sb("BIAS", [P, NG * C])
        OB_IN = sb("OB_IN", [2, C])
        OB_REP = sb("OB_REP", [2, YI, C])
        OB = sb("OB", [P, 2])
        STATS = sb("STATS", [P, B, 6])
        MV = sb("MV", [P, B, 2])
        GM = sb("GM", [P, B, 2])
        NV = sb("NV", [P, B])
        VE = sb("VE", [P, B])
        MASK = CB[:, BASES + 3:BASES + 5]
        BAND = CB[:, BASES + 5:BASES + 5 + YI]
        OWN = CB[:, BASES + 5 + YI:BASES + 5 + 2 * YI]
        REP = CB[:, BASES + 5 + 2 * YI:BASES + 5 + 2 * YI + C]
        NHALF = sb("NHALF", [P, B])
        RS = sb("RS", [P, B])
        NBI = sb("NBI", [P, B])

        flat = S[:, :, :, :, :].rearrange("p a b y w -> p (a b y w)")
        TS = YB * PW

        def carve(k, rows=YB):
            at = int((NB + k) * TS)
            return flat[:, at:at + rows * PW].rearrange("p (y w) -> p y w", w=PW)

        NS1 = [carve(15 + r * (YB + 2) / YB, YB + 2) for r in range(RING)]
        H1 = [carve(6 + r) for r in range(RING)]
        NS = [carve(4), carve(5)]
        NS3 = NS + [carve(1), carve(2)]
        ZERO = carve(0)
        UA = [carve(6 + i) for i in range(3)]
        TA = [carve(9 + i) for i in range(3)]
        TB = [carve(12 + i) for i in range(3)]
        A2 = [carve(15 + i) for i in range(3)]
        B2 = [carve(18 + i) for i in range(3)]
        FT = [carve(21 + i) for i in range(3)]
        assert NB + 24 <= 7 * NB

        PB = [ctx.enter_context(nc.psum_tensor(f"PB{i}", [P, 512], F32)) for i in range(8)]
        OUT_BANK = PB[0:3]
        BUILD_HI, BUILD_LO = PB[3:5], PB[5:7]
        TR_BANK = PB[7]
        RUN = (YB - 1) * PW
        image_tiles = [len(ins) + halo_tiles(ins) for _, ins, _ in cells]
        STAT_BANK = PB[2]
        SEL_IN = flat[0:KC, 3 * NB * TS:3 * NB * TS + TRIPLE * P + NG * 3 * HALO]

        x_loaded = [sem(f"x_loaded{h}") for h in range(HALVES)]
        x_loaded_pool = [sem(f"x_loaded_pool{h}") for h in range(HALVES)]
        single_loaded = sem("single_loaded")
        edges_copied = sem("edges_copied")
        halo_rows = [sem(f"halo_rows{r}") for r in range(RING2)]
        ring_loaded = [sem(f"ring_loaded{r}") for r in range(RING)]
        const_loaded = sem("const_loaded")
        taps_loaded = sem("taps_loaded")
        kan_loaded = sem("kan_loaded")
        kan_ready = sem("kan_ready")
        pool_step = sem("pool_step")
        halo_loaded = [sem("halo_loaded0"), sem("halo_loaded1")]
        w_clear = sem("w_clear")
        hs_clear = sem("hs_clear")
        f_clear = sem("f_clear")
        sel_ready = sem("sel_ready")
        slot_clear = sem("slot_clear")
        pool_const = sem("pool_const")
        bias_rep = sem("bias_rep")
        bias_done = sem("bias_done")
        bias_ready = sem("bias_ready")
        mv_ready = sem("mv_ready")
        group_ready = sem("group_ready")
        nv_ready = sem("nv_ready")
        norm_ready = sem("norm_ready")
        xn_ready = sem("xn_ready")
        columns_round = sem("columns_round")
        dve_step = sem("dve_step")
        act_step = sem("act_step")
        hi_ready = sem("hi_ready")
        lo_ready = sem("lo_ready")
        out_done = sem("out_done")
        evac_done = sem("evac_done")
        tile_used = sem("tile_used")
        added = sem("added")
        pool_norm = sem("pool_norm")
        taps_ready = sem("taps_ready")
        turned = sem("turned")
        turned_hi = sem("turned_hi")
        turned_lo = sem("turned_lo")
        chunk_hi = sem("chunk_hi")
        chunk_lo = sem("chunk_lo")
        w_hi = sem("w_hi")
        w_lo = sem("w_lo")
        basis_u = sem("basis_u")
        basis_a = sem("basis_a")
        basis_b = sem("basis_b")
        basis_b3 = sem("basis_b3")
        feat_ready = sem("feat_ready")
        passed = {name: sem("passed_" + name) for name in ("sp", "pe", "dve", "pool")}
        scratch_clear = sem("scratch_clear")
        out_staged = sem("out_staged")
        stored = sem("stored")
        stored_pool = sem("stored_pool")

        block = ctx.enter_context(nc.Block())
        XV = X[:, :, :].rearrange("p b (y x) -> p b y x", x=WD)
        SV = S[:, :, :, :, 1:WD + 1]
        SF = S[:, :, :, :, :].rearrange("p s b y w -> p s b (y w)")
        HF = HS[:, :, :, :].rearrange("p a y w -> p a (y w)")

        def ximg(b):
            return X[:, bass.ds(b, 1), :].rearrange("p a (y x) -> p (a y) x", x=WD)

        def ximg_flat(b):
            return X[:, bass.ds(b, 1), :].rearrange("p a n -> p (a n)")

        CHUNKS_AT = [(0,), (1,), (2, 3), ()]
        TURN_AT = 2

        def out_bank(outs, o, b):
            return OUT_BANK[o] if len(outs) > 1 else OUT_BANK[b % 2]

        def flat2(a):
            return a.rearrange("p y w -> p (y w)")

        def pass_wait(eng, counter):
            eng.sem_inc(counter, 1)

        def at_half(h, per, n):
            return n if h is None else h * per + n

        PAIR = 2 * FEATS
        ENTRIES = [(par, t) for par in range(2) for t in range(FEATS)]
        EDGES = [(0, FEATS + t) for t in range(HALO_FEATS)]
        BASES_PER_PAIR = 2 * BASES
        PER = FEATS + 3
        FEAT_LAG, HI_LAG, LO_LAG = 2, 3, 4

        BUILD_AT, BUILD_EVAC_AT = 3, 9
        TAIL_AT, UPDATE2_AT, TAIL2_AT, UPDATE_AT = 2, 7, 11, 16

        def halo_part(blk):
            return (slice(0, 3 * HALO), slice(1, WD + 1)) if blk == 1 else (slice(0, HALO), slice(0, PW))

        def image_slice(b):
            return slice(b, b + 1) if isinstance(b, int) else bass.ds(b, 1)

        def sections(eng, lag):
            yield True, 0, range(-EDGE_TILES, PAIR)
            with eng.Fori(1, B // 2) as i:
                yield False, i, range(PAIR)
            if lag:
                yield False, B // 2, range(lag)

        def entry(first, q):
            return EDGES[q + EDGE_TILES] if first and q < 0 else ENTRIES[q % PAIR]

        def bases_to(q):
            tiles = range(0, q + 1) if q >= 0 else range(q + 1, 0)
            n = sum(1 for k in tiles if ENTRIES[k % PAIR][1] < BASES)
            return n if q >= 0 else -n

        def basis_count(first, i, q):
            return i * BASES_PER_PAIR + (EDGE_TILES + (q + 1 if first and q < 0 else bases_to(q)))

        def tile_count(i, q):
            return i * PAIR + (EDGE_TILES + q + 1)

        SPARE = W[0:3 * HALO, 0, :, K3 * NG:MAIN_TILES, :].rearrange("p a t m -> p a (t m)")

        def halo_tile(par, t):
            if par == 0 or t == 0:
                k = t if par == 0 else HALO_FEATS
                return SPARE[:, :, k * TS:(k + 1) * TS]
            return F[0:3 * HALO, RING2 + t - 1].rearrange("p a y w -> p a (y w)")

        def tile_part(first, q, part):
            par, t = entry(first, q)
            if t >= FEATS:
                return halo_tile(par, t - FEATS)[:, part].rearrange("p (y w) -> p y w", w=PW)
            return F[:, q % RING2, part]

        def basis_parts(t):
            return P if t < BASES else (0, 3 * HALO, 3 * HALO, 2 * HALO)[t - BASES]

        LINKS_PER_IMAGE = 5
        PAIR_LINKS = PAIR + 2 * LINKS_PER_IMAGE

        KAN_COLUMNS = FEATS * K3 * C

        def chunk_source(bank, chunk, columns, plain):
            rows, n = (P, columns) if chunk < TRIPLE else (3 * HALO, columns if plain else columns // K3)
            return bank[0:rows, 0:n].rearrange("p (t c) -> p t c", c=C)

        def chunk_parts(part, parity, chunk, n_tiles):
            if chunk < TRIPLE:
                return [(W[:, parity, part, 0:n_tiles, j * C:(j + 1) * C], BAND[:, j:j + 1])
                        for j in range(chunk, YI, TRIPLE)]
            return [(W[0:3 * HALO, parity, part, MAIN_TILES:MAIN_TILES + n_tiles, j * C:(j + 1) * C],
                     MASK[0:3 * HALO, side:side + 1]) for side, j in ((0, 0), (1, YI - 1))]

        LAYERS = [(len(ins), [group for group, _ in outs]) for _, ins, outs in cells]
        LAYERS.append(LAYERS[0])
        CELL_COLUMNS = [n_in * K3 * len(groups) * C for n_in, groups in LAYERS]
        SINGLE_OUTS = len(LAYERS[NC][1])

        @block.sync
        def _(sp):
            xv = x.rearrange("b c (yb yi) w -> b yi c yb w", yi=YI)
            for b in range(B):
                for yi in range(X_SPLIT):
                    sp.dma_start(XV[C * yi:C * (yi + 1), b], xv[b, yi]).then_inc(x_loaded[b // NB], 16)
            sp.dma_start(RAW_ONE[0][:, :], l1w.rearrange("o i k d -> o (i k d)")).then_inc(single_loaded, 16)
            sp.dma_start(RAW_ONE[1][:, :], l3w).then_inc(single_loaded, 16)

            def wait_both(sem_a, a, sem_b, b):
                sp.wait_ge(sem_a, a)
                pass_wait(sp, passed["sp"])
                sp.wait_ge(sem_b, b)
                pass_wait(sp, passed["sp"])

            def load_taps(k):
                sp.dma_start(RAW[:, :], l0w[k // 4, k % 4].rearrange("o i k d -> o (i k d)"))\
                  .then_inc(taps_loaded, 16)

            sp.wait_ge(hs_clear, 1)
            sp.wait_ge(taps_ready, 1)
            load_taps(1)
            with sp.Fori(0, HALVES) as h:
                for k, (_, ins, outs) in enumerate(cells):
                    for b in range(NB):
                        par = b % 2
                        if k == 0:
                            written, n = xn_ready, h * NB + (b + 1)
                        else:
                            written, n = evac_done, h * OH + (outs_before[k - 1] + (b + 1) * len(cells[k - 1][2]))
                        if b >= 2:
                            wait_both(written, n, lo_ready, h * TH + (tiles_before[k] + (b - 1) * image_tiles[k]))
                        elif k:
                            before = tiles_before[k] - (1 - b) * image_tiles[k - 1]
                            wait_both(written, n, lo_ready, h * TH + before)
                        else:
                            sp.wait_ge(written, n)
                        if len(ins) == NG:
                            for g, s in enumerate(ins):
                                top, bot = HALO * g, HALO * g + C
                                sp.dma_start(HF[top:top + C, par * 2, PW:YB * PW],
                                             SF[P - C:P, s, b, 0:RUN]).then_inc(halo_loaded[par], 16)
                                sp.dma_start(HF[bot:bot + C, par * 2, 0:RUN],
                                             SF[0:C, s, b, PW:YB * PW]).then_inc(halo_loaded[par], 16)
                        else:
                            slots = slice(ins[0], ins[-1] + 1, max(ins[-1] - ins[0], 1))
                            bufs = slice(par * 2, par * 2 + len(ins))
                            for dx in range(K3):
                                top, bot = HALO * dx, HALO * dx + C
                                sp.dma_start(HF[top:top + C, bufs, PW + 1:YB * PW - 1],
                                             SF[P - C:P, slots, b, dx:dx + RUN - 2]).then_inc(halo_loaded[par], 16)
                                sp.dma_start(HF[bot:bot + C, bufs, 1:RUN - 1],
                                             SF[0:C, slots, b, PW + dx:PW + dx + RUN - 2])\
                                  .then_inc(halo_loaded[par], 16)
                        if b == 0:
                            sp.wait_ge(taps_ready, h * NC + (k + 2))
                            pass_wait(sp, passed["sp"])
                            load_taps((k + 2) % NC)

            def halo_block(blk, r):
                src = flat2(NS1[r] if blk == 1 else NS3[r])
                dst = flat2(H1[r]) if blk == 1 else HF[:, r]
                pieces = []
                if blk == 3:
                    pieces += [(dst[0:C, PW:YB * PW], src[P - C:P, 0:RUN]), (dst[C:HALO, 0:RUN], src[0:C, PW:YB * PW])]
                else:
                    for g in range(K3):
                        top, bot, n = HALO * g, HALO * g + C, YB * PW - 2
                        pieces += [(dst[top:top + C, 1:1 + n], src[P - C:P, g:g + n]),
                                   (dst[bot:bot + C, 1:1 + n], src[0:C, 2 * PW + g:2 * PW + g + n])]
                for to, source in pieces:
                    sp.dma_start(to, source).then_inc(ring_loaded[r], 16)

            ov = out.rearrange("b c (yb yi) w -> b yi c yb w", yi=YI)

            for b in range(B):
                sp.wait_ge(xn_ready, B + b + 1)
                if b >= RING:
                    sp.wait_ge(lo_ready, T_AT[0] + ORDER_AT["halo", b - RING])
                halo_block(1, b % RING)

            sp.wait_ge(lo_ready, T_AT[1] + EDGE_TILES)
            for t in range(HALO_FEATS):
                sp.dma_start(halo_tile(1, t).bitcast(F32), halo_tile(0, t).bitcast(F32)).then_inc(edges_copied, 16)
            sp.wait_ge(edges_copied, 16 * HALO_FEATS)
            for first, i, tiles in sections(sp, 0):
                for q in tiles:
                    if q < 0:
                        continue
                    par, t = ENTRIES[q]
                    sp.wait_ge(lo_ready, T_AT[1] + tile_count(i, q))
                    pass_wait(sp, passed["sp"])
                    if not first:
                        sp.wait_ge(tile_used, i * (2 * PER) + ((par - 2) * PER + FEATS + t // HALO_FEATS + 1))
                        pass_wait(sp, passed["sp"])
                    src = F[:, q % RING2].rearrange("p a y w -> p a (y w)").bitcast(F32)
                    dst = halo_tile(par, t // HALO_FEATS).bitcast(F32)
                    top, bot = HALO * (t % HALO_FEATS), HALO * (t % HALO_FEATS) + C
                    sp.dma_start(dst[top:top + C, :, PW:YB * PW], src[P - C:P, :, 0:RUN])\
                      .then_inc(halo_rows[q % RING2], 16)
                    sp.dma_start(dst[bot:bot + C, :, 0:RUN], src[0:C, :, PW:YB * PW])\
                      .then_inc(halo_rows[q % RING2], 16)

            for b in range(B + 3):
                if b < B:
                    sp.wait_ge(xn_ready, 3 * B + b + 1)
                    sp.wait_ge(lo_ready, T_AT[2] + (ORDER_AT["halo", b - RING] if b >= RING else 0))
                    halo_block(3, b % RING)
                if b >= 3:
                    sp.wait_ge(out_staged, b - 2)
                    for yi in range(OUT_SPLIT):
                        sp.dma_start(ov[b - 3, yi], XV[C * yi:C * (yi + 1), b - 3]).then_inc(stored, 16)
            sp.wait_ge(stored, B * OUT_SPLIT * 16)

        @block.gpsimd
        def _(pool):
            def rearrange_taps(kind, n):
                if n:
                    pool.wait_ge(turned, n)
                if kind == "cell":
                    pool.wait_ge(taps_loaded, (n + 1) * 16)
                    dst = RAWR[:, :, :].rearrange("o (g d) (k c) -> o g d k c", g=NG, c=C)
                    src = RAW[:, :].rearrange("o (g c k d) -> o g d k c", g=NG, c=C, k=K3)
                    for g in range(NG):
                        last = pool.tensor_copy(dst[:, g], src[:, g])
                elif kind == "circular":
                    pool.wait_ge(single_loaded, 32)
                    dst = RAWR[0:C, 0:K3].rearrange("o d (k c) -> o d k c", c=C)
                    src = RAW_ONE[0][:, :].rearrange("o (c k d) -> o d k c", c=C, k=K3)
                    for dx in range(K3):
                        for ky in range(K3):
                            last = pool.tensor_copy(dst[:, dx, ky], src[:, K3 - 1 - dx, K3 - 1 - ky])
                else:
                    dst = RAWR[0:C, 0:K3].rearrange("o d (k c) -> o d k c", c=C)
                    last = pool.tensor_copy(dst, RAW_ONE[1][:, :].rearrange("o (k d c) -> o d k c", k=K3, c=C))
                last.then_inc(taps_ready, 1)

            for par in range(2):
                for part in range(2):
                    last = pool.memset(W[0:3 * HALO, par, part, MAIN_TILES:TILES, :].bitcast(F32), 0.0)
            last.then_inc(w_clear, 1)
            xv = x.rearrange("b c (yb yi) w -> b yi c yb w", yi=YI)
            for b in range(B):
                for yi in range(X_SPLIT, YI):
                    pool.dma_start(XV[C * yi:C * (yi + 1), b], xv[b, yi]).then_inc(x_loaded_pool[b // NB], 16)
                if b == 1:
                    rearrange_taps("cell", 0)
            pool.memset(NHALF[:, :], -0.5).then_inc(pool_const, 1)
            pool.wait_ge(pool_const, 1)

            def norm(cols, images, n):
                pool.wait_ge(nv_ready, n)
                pass_wait(pool, passed["pool"])
                pool.tensor_tensor(RS[:, images], VE[:, cols], NHALF[:, cols], ALU.pow).then_inc(pool_norm, 1)
                pool.wait_ge(pool_norm, n)
                pass_wait(pool, passed["pool"])
                pool.tensor_tensor(NBI[:, images], GM[:, cols, 0], RS[:, images], ALU.mult).then_inc(norm_ready, 1)

            o0 = 0
            o1 = o0 + NJ * 81 * BASES
            o2 = o1 + NJ * 81
            o3 = o2 + NJ * 81
            assert o3 + FEATS * 9 * NJ <= NB * TS
            SPL = flat[:, o0:o1].rearrange("o (j a n s) -> o j a n s", j=NJ, a=9, n=9)
            SPF = flat[:, o0:o1].rearrange("o (q s) -> o q s", s=BASES)
            SCL = flat[:, o1:o2]
            BAS = flat[:, o2:o3]
            BAV = BAS.rearrange("o (j a n) -> o j a n", j=NJ, a=9)
            SUM = SPF.rearrange("o (j a n) s -> o j a (n s)", j=NJ, a=9)
            TWO = flat[:, o3:o3 + FEATS * 9 * NJ].rearrange("o (q j) -> o q j", j=NJ)

            def load_kan():
                for g in range(C // NJ):
                    js, rows = slice(g * NJ, (g + 1) * NJ), slice(C * g, C * (g + 1))
                    pool.dma_start(flat[rows, o0:o1],
                                   l2spline[:, js].rearrange("o j a n s -> o (j a n s)")).then_inc(kan_loaded, 16)
                    pool.dma_start(SCL[rows], l2scale[:, js].rearrange("o j a n -> o (j a n)"))\
                        .then_inc(kan_loaded, 16)
                    pool.dma_start(BAS[rows], l2base[:, js].rearrange("o j a n -> o (j a n)")).then_inc(kan_loaded, 16)

            def kan_taps():
                pool.wait_ge(kan_loaded, 3 * 16 * (C // NJ))
                scl = SCL.rearrange("o (q s) -> o q s", s=1).broadcast_to([P, NJ * 81, BASES])
                pool.tensor_tensor(SPF, SPF, scl, ALU.mult).then_inc(pool_step, 1)
                steps = 1
                for a in range(1, 9):
                    pool.wait_ge(pool_step, steps)
                    pool.tensor_tensor(SUM[:, :, 0], SUM[:, :, 0], SUM[:, :, a], ALU.add).then_inc(pool_step, 1)
                    pool.tensor_tensor(BAV[:, :, 0], BAV[:, :, 0], BAV[:, :, a], ALU.add).then_inc(pool_step, 1)
                    steps += 2
                pool.wait_ge(pool_step, steps)
                n = BASES * 9
                for j in range(NJ):
                    dst = TWO[:, 0:n, j].rearrange("o (s d k) -> o s d k", s=BASES, d=K3)
                    src = SPL[:, j, 0].rearrange("o (k d) s -> o s d k", d=K3)
                    pool.tensor_scalar(dst, src, -1.0 / 6.0, None, ALU.mult)
                    dst = TWO[:, n:n + 9, j].rearrange("o (d k) -> o d k", d=K3)
                    last = pool.tensor_copy(dst, BAV[:, j, 0].rearrange("o (k d) -> o d k", d=K3))
                last.then_inc(pool_step, 1)
                pool.wait_ge(pool_step, steps + 1)
                kan = KAN[:, :, :].rearrange("o q (k c) -> o (q k) c", c=C)
                for g in range(C // NJ):
                    last = pool.tensor_scalar(kan[:, :, g * NJ:(g + 1) * NJ], TWO, OWN[:, g:g + 1], None, ALU.mult)
                last.then_inc(kan_ready, 1)

            norm(slice(0, B), slice(0, B), 1)
            pool.wait_ge(sel_ready, 1)
            for col in (0, WD + 1):
                last = pool.memset(S[:, 3, :, :, col:col + 1], 0.0)
            last.then_inc(slot_clear, 1)
            rearrange_taps("cell", 1)
            last_reader = max(k for k, (_, ins, _) in enumerate(cells) if 0 in ins)
            for h in range(HALVES):
                for n in range(h * NC + 2, (h + 1) * NC + 2):
                    if n < HALVES * NC:
                        rearrange_taps("cell", n)
                    elif n == HALVES * NC:
                        rearrange_taps("circular", n)
                    if n == (HALVES - 1) * NC + last_reader + 3:
                        pool.wait_ge(evac_done, h * OH + outs_before[last_reader + 1])
                        load_kan()
                    if n == HALVES * NC:
                        kan_taps()
                        pool.wait_ge(evac_done, h * OH + outs_before[NC - 1])
                        for image in NS3:
                            for col in (0, WD + 1):
                                pool.memset(image[:, :, col:col + 1], 0.0)
                        pool.memset(ZERO, 0.0).then_inc(scratch_clear, 1)
                with pool.Fori(0, NB // 2) as i:
                    for par in range(2):
                        norm(slice(par, par + 1), bass.ds(i * 2 + (h * NB + par), 1), i * 2 + (h * NB + par + 2))
            rearrange_taps("conv", FILL_AT[1])
            with pool.Fori(0, B // 2) as i:
                for par in range(2):
                    norm(slice(par, par + 1), bass.ds(i * 2 + par, 1), i * 2 + (2 + par + B))
            for first, i, tiles in sections(pool, TAIL2_AT + 3):
                for q in tiles:
                    if q == TAIL_AT + 2 and not first:
                        norm(slice(0, 1), image_slice(i * 2 - 2), i * 2 + (2 + 2 * B - 2))
                    if q == TAIL2_AT + 2 and not first:
                        norm(slice(1, 2), image_slice(i * 2 - 1), i * 2 + (2 + 2 * B - 1))
                    t = entry(first, q)[1]
                    if t == BASES or i is B // 2:
                        continue
                    pt, n = basis_parts(t), basis_count(first, i, q)
                    pool.wait_ge(basis_a, n)
                    pool.tensor_tensor(A2[q % 3][0:pt], A2[q % 3][0:pt], TA[q % 3][0:pt], ALU.mult)
                    pool.wait_ge(basis_b, n)
                    pool.tensor_tensor(TB[q % 3][0:pt], TB[q % 3][0:pt], B2[q % 3][0:pt], ALU.mult)\
                        .then_inc(basis_b3, 1)


            ov = out.rearrange("b c (yb yi) w -> b yi c yb w", yi=YI)
            for b in range(B):
                pool.wait_ge(out_staged, b + 1)
                for yi in range(OUT_SPLIT, YI):
                    pool.dma_start(ov[b, yi], XV[C * yi:C * (yi + 1), b]).then_inc(stored_pool, 16)
            pool.wait_ge(stored_pool, B * (YI - OUT_SPLIT) * 16)

        def basis_act(act, normalise, banded):
            act.wait_ge(out_done, O_AT[3])
            for first, i, tiles in sections(act, HI_LAG):
                for e in tiles:
                    if first and e == BUILD_EVAC_AT:
                        banded(CELL_COLUMNS[NC], 0, None, C_AT[2], plain=True)
                    if not i is B // 2:
                        par, t = entry(first, e)
                        if t == 0:
                            if not first:
                                act.wait_ge(feat_ready, tile_count(i, (par - 1) * FEATS - 1))
                            normalise(NS[par][:, :, 1:WD + 1], i * 2 + par, i * 2 + (par + 2 + B)).then_inc(xn_ready, 1)
                            act.wait_ge(xn_ready, i * 2 + (2 * B + par + 1))
                        src, parts = (NS[par], P) if t < FEATS else (ZERO, 3 * HALO)
                        if not (first and e - 4 < -EDGE_TILES):
                            act.wait_ge(feat_ready, tile_count(i, e - 4))
                        elif e - 3 == -EDGE_TILES:
                            act.wait_ge(feat_ready, tile_count(i, e - 3))
                        u, tb, b2 = UA[e % 3], TB[e % 3], B2[e % 3]
                        pt = basis_parts(t)
                        if pt:
                            col = t if t < BASES else t - 1
                            last = act.activation(u[0:pt], src[0:pt], ACT.Abs, scale=2.5, bias=CB[0:pt, col:col + 1])
                        if pt < parts:
                            last = act.activation(u[pt:parts], src[pt:parts], ACT.Tanh, scale=0.5)
                        last.then_inc(basis_u, 1)
                        if pt:
                            n = basis_count(first, i, e)
                            act.wait_ge(basis_u, tile_count(i, e))
                            if not (first and e - 3 < -EDGE_TILES):
                                act.wait_ge(feat_ready, tile_count(i, e - 3))
                            act.activation(tb[0:pt], u[0:pt], ACT.Relu, scale=-1.0, bias=1.0).then_inc(act_step, 1)
                    q = e - HI_LAG
                    if not (first and q < -EDGE_TILES):
                        t = entry(first, q)[1]
                        parts = P if t < FEATS else 3 * HALO
                        if t < FEATS and not (first and q < RING2):
                            k, use = q - RING2, q // RING2
                            act.wait_ge(tile_used, i * (2 * PER) + (k // FEATS * PER + k % FEATS + 1))
                            act.wait_ge(halo_rows[q % RING2], i * (PAIR // RING2 * 32) + use * 32)
                        act.wait_ge(feat_ready, tile_count(i, q))
                        act.activation(tile_part(first, q, 0), FT[q % 3][0:parts], ACT.Copy).then_inc(hi_ready, 1)
                    if not i is B // 2 and pt:
                        act.wait_ge(act_step, n)
                        act.activation(b2[0:pt], tb[0:pt], ACT.Square).then_inc(basis_b, 1)

        @block.scalar
        def _(act):
            act.dma_start(SEL_IN, consts[0:KC, P + NG * C + CB_COLUMNS:]).then_inc(const_loaded, 16)
            act.dma_start(IDF[:, :], consts[0:NG * C, P:P + NG * C]).then_inc(const_loaded, 16)
            act.dma_start(RAW[:, :], l0w[0, 0].rearrange("o i k d -> o (i k d)")).then_inc(taps_loaded, 16)
            act.dma_start(CB[:, :], consts[:, P + NG * C:P + NG * C + CB_COLUMNS]).then_inc(const_loaded, 16)
            act.dma_start(G[:, :], consts[:, 0:P]).then_inc(const_loaded, 16)
            act.dma_start(BN_IN[:, :], l0b.rearrange("a r (g c) -> (a r g) c", c=C)).then_inc(const_loaded, 16)
            act.dma_start(OB_IN[0:1, :], l2bias.rearrange("(a c) -> a c", a=1)).then_inc(const_loaded, 16)
            act.dma_start(OB_IN[1:2, :], l3bias.rearrange("(a c) -> a c", a=1)).then_inc(const_loaded, 16)
            act.wait_ge(const_loaded, 112)
            act.activation(SEL[:, :], SEL_IN, ACT.Copy).then_inc(sel_ready, 1)

            def turned_hi_part(columns, n):
                act.wait_ge(turned, n)
                act.activation(WT[:, 0, 0:columns], TR_BANK[0:KC, 0:columns], ACT.Copy).then_inc(turned_hi, 1)

            def banded(columns, parity, h, at, chunks=range(CHUNKS), plain=False):
                for c in chunks:
                    act.wait_ge(chunk_hi, at_half(h, CH, at + c + 1))
                    src = chunk_source(BUILD_HI[(at + c) % 2], c, columns, plain)
                    for dst, mask in chunk_parts(0, parity, c, src.shape[1]):
                        last = act.activation(dst, src, ACT.Copy, scale=mask)
                    last.then_inc(w_hi, 1)

            def normalise(dst, b, n):
                act.wait_ge(norm_ready, n)
                return act.activation(dst, ximg(b), ACT.Identity, bias=NBI[:, bass.ds(b, 1)],
                                      scale=RS[:, bass.ds(b, 1)])

            def split_hi(h, k, b):
                ins = cells[k][1]
                par = b % 2
                if k == 0:
                    act.wait_ge(xn_ready, h * NB + (b + 1))
                else:
                    act.wait_ge(evac_done, h * OH + (outs_before[k - 1] + (b + 1) * len(cells[k - 1][2])))
                if b >= 2:
                    act.wait_ge(out_done, h * OH + (outs_before[k] + (b - 1) * len(cells[k][2])))
                elif k:
                    act.wait_ge(out_done, h * OH + (outs_before[k] - (1 - b) * len(cells[k - 1][2])))
                for g, s in enumerate(ins):
                    act.activation(F[:, par * 4 + g, 0, :, 1:WD + 1], SV[:, s, b], ACT.Copy)\
                       .then_inc(hi_ready, 1)
                n = len(ins)
                loads = halo_before[k] + (b // 2 + 1) * halo_dmas(ins) * 16
                act.wait_ge(halo_loaded[par], h * HH + loads)
                for t in range(halo_tiles(ins)):
                    act.activation(F[0:3 * HALO, par * 4 + n + t, 0, :, 1:WD + 1],
                                   HS[:, par * 2 + t, :, 1:WD + 1], ACT.Copy).then_inc(hi_ready, 1)

            act.wait_ge(f_clear, 1)
            act.wait_ge(w_clear, 1)
            turned_hi_part(CELL_COLUMNS[0], 1)
            banded(CELL_COLUMNS[0], 0, None, 0)
            with act.Fori(0, HALVES) as h:
                for b in range(NB):
                    normalise(SV[:, 0, b], h * NB + b, 1).then_inc(xn_ready, 1)
                turned_hi_part(CELL_COLUMNS[1], h * NC + 2)
                split_hi(h, 0, 0)
                for k, (cell, ins, outs) in enumerate(cells):
                    if k == 3:
                        act.wait_ge(slot_clear, 1)
                    for b in range(NB):
                        if b + 1 < NB:
                            split_hi(h, k, b + 1)
                        elif k + 1 < NC:
                            split_hi(h, k + 1, 0)
                        for o, (group, slot) in enumerate(outs):
                            act.wait_ge(out_done, h * OH + (outs_before[k] + b * len(outs) + o + 1))
                            act.activation(SV[:, slot, b],
                                           out_bank(outs, o, b)[:, :].rearrange("p (y x) -> p y x", x=WD), ACT.Relu,
                                           bias=BIAS[:, cell * NG + group:cell * NG + group + 1])\
                               .then_inc(evac_done, 1)
                        banded(CELL_COLUMNS[k + 1], (k + 1) % 2, h, chunks_before[k + 1], CHUNKS_AT[b])
                        if b == TURN_AT and k + 2 <= NC:
                            turned_hi_part(CELL_COLUMNS[k + 2], h * NC + (k + 3))

            def split_rows(blk, b):
                r = b % RING
                dst = NS1[r] if blk == 1 else NS3[r]
                if b >= RING:
                    act.wait_ge(out_done, O_AT[blk] + b - RING + 1)
                elif blk == 1:
                    act.wait_ge(out_done, O_AT[1] - (1 if b < RING // 2 else 0))
                else:
                    for slot in (2 * r, 2 * r + 1):
                        if slot < RING2:
                            last_use = PAIR - RING2 + slot
                            act.wait_ge(tile_used, (B - 1) * PER + last_use % FEATS + 1)
                            act.wait_ge(halo_rows[slot], B // 2 * PAIR // RING2 * 32)
                        else:
                            act.wait_ge(tile_used, B * PER)
                rows = slice(1, YB + 1) if blk == 1 else slice(0, YB)
                last = normalise(dst[:, rows, 1:WD + 1], b, b + (2 + (blk - 1) * B))
                if blk == 1:
                    for col, src in ((0, WD - 1), (WD + 1, 0)):
                        last = act.activation(dst[:, rows, col:col + 1], ximg(b)[:, :, src:src + 1], ACT.Identity,
                                              bias=NBI[:, bass.ds(b, 1)], scale=RS[:, bass.ds(b, 1)])
                    last.then_inc(columns_round, 1)
                    act.wait_ge(columns_round, b + 1)
                    for row, src in ((0, YB), (YB + 1, 1)):
                        last = act.activation(dst[:, row:row + 1], dst[:, src:src + 1], ACT.Copy)
                last.then_inc(xn_ready, 1)
                act.wait_ge(xn_ready, b + (blk * B + 1))
                act.activation(F[:, r * 2, 0], dst[:, rows], ACT.Copy).then_inc(hi_ready, 1)

            def split_halo(blk, b):
                r = b % RING
                halo = H1[r] if blk == 1 else HS[:, r]
                loads = B // RING * 2 * K3 + (b // RING + 1) * 2 if blk == 3 else (b // RING + 1) * 2 * K3
                act.wait_ge(ring_loaded[r], loads * 16)
                rows, cols = halo_part(blk)
                act.activation(F[rows, r * 2 + 1, 0, :, cols], halo[rows, :, cols], ACT.Copy)\
                   .then_inc(hi_ready, 1)

            act.wait_ge(scratch_clear, 1)
            act.wait_ge(added, B - 2)
            for tile, b in ORDER:
                split_rows(1, b) if tile == "rows" else split_halo(1, b)
                if (tile, b) == ORDER[KAN_AFTER]:
                    turned_hi_part(KAN_COLUMNS, FILL_AT[1] + 1)
                    banded(KAN_COLUMNS, 1, None, C_AT[1])
                    turned_hi_part(CELL_COLUMNS[NC], FILL_AT[2] + 1)
            basis_act(act, normalise, banded)
            for tile, b in ORDER:
                split_rows(3, b) if tile == "rows" else split_halo(3, b)

        @block.vector
        def _(dve):
            steps = Count()

            nc.vector.memset(HS[:, :, :, :], 0.0).then_inc(hs_clear, 1)
            edges = F[:, :, :, :, :].bitcast(F32).rearrange("p s a y w -> p (s a y) w")
            for col in (0, WD + 1):
                nc.vector.memset(edges[:, :, col:col + 1], 0.0)
                for slots in (slice(0, 3), slice(4, 7)):
                    for s in range(slots.start, slots.stop):
                        last = nc.vector.memset(S[:, s, :, :, col:col + 1], 0.0)
            last.then_inc(f_clear, 1)

            dve.wait_ge(const_loaded, 112)
            for yi in range(YI):
                nc.vector.tensor_copy(BN_REP[:, yi], BN_IN[:, :])
                last = nc.vector.tensor_copy(OB_REP[:, yi], OB_IN[:, :])
            last.then_inc(bias_rep, 1)

            def turned_lo_part(columns, n):
                dve.wait_ge(turned_hi, n)
                nc.vector.tensor_tensor(WT[:, 1, 0:columns], TR_BANK[0:KC, 0:columns],
                                        WT[:, 0, 0:columns].bitcast(F32), ALU.subtract).then_inc(turned_lo, 1)

            def banded(columns, parity, h, at, chunks=range(CHUNKS), plain=False):
                for c in chunks:
                    dve.wait_ge(chunk_lo, at_half(h, CH, at + c + 1))
                    src = chunk_source(BUILD_LO[(at + c) % 2], c, columns, plain)
                    for dst, mask in chunk_parts(1, parity, c, src.shape[1]):
                        last = nc.vector.tensor_scalar(dst, src, mask, None, ALU.mult)
                    last.then_inc(w_lo, 1)

            turned_lo_part(CELL_COLUMNS[0], 1)
            dve.wait_ge(w_clear, 1)
            banded(CELL_COLUMNS[0], 0, None, 0)

            for b in range(B):
                if b % NB == 0:
                    dve.wait_ge(x_loaded[b // NB], 16 * X_SPLIT * NB)
                    dve.wait_ge(x_loaded_pool[b // NB], 16 * (YI - X_SPLIT) * NB)
                last = nc.vector.bn_stats(STATS[:, b], X[:, b])
            last.then_inc(dve_step, 1)
            dve.wait_ge(dve_step, steps.next())
            for b in range(B):
                last = nc.vector.bn_aggr(MV[:, b], STATS[:, b])
            last.then_inc(dve_step, 1)
            dve.wait_ge(dve_step, steps.next())

            def squares(cols):
                m, v = MV[:, cols, 0], MV[:, cols, 1]
                nc.vector.tensor_tensor(NV[:, cols], m, m, ALU.mult).then_inc(dve_step, 1)
                dve.wait_ge(dve_step, steps.next())
                nc.vector.scalar_tensor_tensor(v, v, GN_EPS, NV[:, cols], ALU.add, ALU.add).then_inc(mv_ready, 1)

            def group_stats(cols, n):
                dve.wait_ge(group_ready, n)
                g = GM[:, cols, :].rearrange("p b a -> p (b a)")
                nc.vector.tensor_scalar(g, STAT_BANK[:, 2 * cols.start:2 * cols.stop], -1.0, None, ALU.mult)\
                    .then_inc(dve_step, 1)
                dve.wait_ge(dve_step, steps.next())
                m, v = GM[:, cols, 0], GM[:, cols, 1]
                nc.vector.tensor_tensor(NV[:, cols], m, m, ALU.mult).then_inc(dve_step, 1)
                dve.wait_ge(dve_step, steps.next())
                nc.vector.scalar_tensor_tensor(VE[:, cols], NV[:, cols], -1.0, v, ALU.mult, ALU.subtract)\
                    .then_inc(nv_ready, 1)

            def image_stats(b, par):
                nc.vector.bn_stats(STATS[:, par], ximg_flat(b)).then_inc(dve_step, 1)
                dve.wait_ge(dve_step, steps.next())
                pass_wait(dve, passed["dve"])
                nc.vector.bn_aggr(MV[:, par], STATS[:, par]).then_inc(dve_step, 1)
                dve.wait_ge(dve_step, steps.next())
                squares(slice(par, par + 1))

            squares(slice(0, B))
            group_stats(slice(0, B), 1)
            dve.wait_ge(bias_done, 1)
            nc.vector.tensor_copy(BIAS[:, :], OUT_BANK[0][:, 0:NG * C])
            nc.vector.tensor_copy(OB[:, :], OUT_BANK[0][:, 64:66]).then_inc(bias_ready, 1)

            def split_lo(h, k, b):
                ins = cells[k][1]
                par, n = b % 2, len(ins)
                at = tiles_before[k] + b * image_tiles[k]
                for g, s in enumerate(ins):
                    dve.wait_ge(hi_ready, h * TH + (at + g + 1))
                    nc.vector.tensor_tensor(F[:, par * 4 + g, 1, :, 1:WD + 1], SV[:, s, b],
                                            F[:, par * 4 + g, 0, :, 1:WD + 1].bitcast(F32), ALU.subtract)\
                        .then_inc(lo_ready, 1)
                for t in range(halo_tiles(ins)):
                    slot = par * 4 + n + t
                    dve.wait_ge(hi_ready, h * TH + (at + n + t + 1))
                    nc.vector.tensor_tensor(F[0:3 * HALO, slot, 1, :, 1:WD + 1], HS[:, par * 2 + t, :, 1:WD + 1],
                                            F[0:3 * HALO, slot, 0, :, 1:WD + 1].bitcast(F32), ALU.subtract)\
                        .then_inc(lo_ready, 1)

            def tail(b, par, blk):
                dve.wait_ge(norm_ready, b + (1 + blk * B))
                group_stats(slice(par, par + 1), b + (2 + blk * B))

            half_links = NB * LINKS_PER_IMAGE
            links0 = steps.n + steps.base
            with dve.Fori(0, HALVES) as h:
                steps.enter(h * half_links + links0)
                turned_lo_part(CELL_COLUMNS[1], h * NC + 2)
                split_lo(h, 0, 0)
                for k, (cell, ins, outs) in enumerate(cells):
                    for b in range(NB):
                        if b + 1 < NB:
                            split_lo(h, k, b + 1)
                        elif k + 1 < NC:
                            split_lo(h, k + 1, 0)
                        banded(CELL_COLUMNS[k + 1], (k + 1) % 2, h, chunks_before[k + 1], CHUNKS_AT[b])
                        if b == TURN_AT and k + 2 <= NC:
                            turned_lo_part(CELL_COLUMNS[k + 2], h * NC + (k + 3))
                        if k == NC - 1:
                            img = h * NB + b
                            dve.wait_ge(evac_done, h * OH + (outs_before[k] + b + 1))
                            nc.vector.tensor_tensor(ximg(img), ximg(img), SV[:, outs[0][1], b], ALU.add)\
                                .then_inc(added, 1)
                            dve.wait_ge(added, img + 1)
                            pass_wait(dve, passed["dve"])
                            image_stats(img, b % 2)
                            if b:
                                tail(h * NB + (b - 1), (b - 1) % 2, 0)
                tail(h * NB + (NB - 1), (NB - 1) % 2, 0)
                assert steps.n == half_links
            steps.enter(links0 + HALVES * half_links)

            def split_rows(blk, b):
                r = b % RING
                src = NS1[r][:, 1:YB + 1] if blk == 1 else NS3[r]
                dve.wait_ge(hi_ready, T_AT[blk - 1] + ORDER_AT["rows", b])
                nc.vector.tensor_tensor(F[:, r * 2, 1], src, F[:, r * 2, 0].bitcast(F32), ALU.subtract)\
                    .then_inc(lo_ready, 1)

            def split_halo(blk, b):
                r = b % RING
                halo = H1[r] if blk == 1 else HS[:, r]
                dve.wait_ge(hi_ready, T_AT[blk - 1] + ORDER_AT["halo", b])
                rows, cols = halo_part(blk)
                nc.vector.tensor_tensor(F[rows, r * 2 + 1, 1, :, cols], halo[rows, :, cols],
                                        F[rows, r * 2 + 1, 0, :, cols].bitcast(F32), ALU.subtract)\
                    .then_inc(lo_ready, 1)

            def update(blk, b, par):
                if blk == 2:
                    dve.wait_ge(tile_used, b * PER + PER)
                else:
                    dve.wait_ge(out_done, b + (O_AT[blk] + 1))
                psum, ximage = OUT_BANK[par][:, :], ximg_flat(b)
                if blk == 1:
                    nc.vector.tensor_tensor(ximage, psum, ximage, ALU.add).then_inc(added, 1)
                elif blk == 2:
                    nc.vector.scalar_tensor_tensor(ximage, psum, OB[:, 0:1], ximage, ALU.add, ALU.add)\
                        .then_inc(added, 1)
                else:
                    nc.vector.scalar_tensor_tensor(ximage, psum, OB[:, 1:2], ximage, ALU.add, ALU.add)\
                        .then_inc(out_staged, 1)
                if blk < 3:
                    dve.wait_ge(added, b + (blk * B + 1))
                    pass_wait(dve, passed["dve"])
                    image_stats(b, par)

            for n, (tile, b) in enumerate(ORDER):
                if tile == "rows":
                    split_rows(1, b)
                else:
                    split_halo(1, b)
                    if b >= 1:
                        update(1, b - 1, (b - 1) % 2)
                    if b >= 2:
                        tail(b - 2, b % 2, 1)
                if n == KAN_AFTER:
                    turned_lo_part(KAN_COLUMNS, FILL_AT[1] + 1)
                    banded(KAN_COLUMNS, 1, None, C_AT[1])
                    turned_lo_part(CELL_COLUMNS[NC], FILL_AT[2] + 1)
            update(1, B - 1, 1)
            tail(B - 2, 0, 1)
            tail(B - 1, 1, 1)

            links2 = None
            for first, i, tiles in sections(dve, LO_LAG):
                if not first:
                    if links2 is None:
                        links2 = steps.n + steps.base
                    steps.enter((i - 1) * PAIR_LINKS + links2)
                last_section = i is B // 2
                for e in tiles:
                    if first and e == BUILD_EVAC_AT:
                        banded(CELL_COLUMNS[NC], 0, None, C_AT[2], plain=True)
                    if not last_section:
                        t = entry(first, e)[1]
                        pt = basis_parts(t)
                        parts = P if t < FEATS else 3 * HALO
                        u, a, a2 = UA[e % 3], TA[e % 3], A2[e % 3]
                        dve.wait_ge(basis_u, tile_count(i, e))
                        if not (first and e - 3 < -EDGE_TILES):
                            dve.wait_ge(feat_ready, tile_count(i, e - 3))
                        if pt:
                            last = nc.vector.tensor_scalar(a[0:pt], u[0:pt], 2.0, 2.0, ALU.min, ALU.subtract)
                        if pt < parts:
                            last = nc.vector.tensor_scalar(a[pt:parts], u[pt:parts], 0.5, 0.5, ALU.mult, ALU.add)
                        last.then_inc(dve_step, 1)
                    q = e - FEAT_LAG
                    if not (first and q < -EDGE_TILES) and not (last_section and q >= 0):
                        par, t = entry(first, q)
                        pt = basis_parts(t)
                        parts, src = (P, NS[par]) if t < FEATS else (3 * HALO, ZERO)
                        if not (first and q - 3 < -EDGE_TILES):
                            dve.wait_ge(lo_ready, T_AT[1] + tile_count(i, q - 3))
                        if pt < parts:
                            last = nc.vector.tensor_tensor(FT[q % 3][pt:parts], TA[q % 3][pt:parts], src[pt:parts],
                                                           ALU.mult)
                        if pt:
                            dve.wait_ge(basis_b3, basis_count(first, i, q))
                            last = nc.vector.scalar_tensor_tensor(
                                flat2(FT[q % 3])[0:pt], flat2(TB[q % 3])[0:pt], 4.0, flat2(A2[q % 3])[0:pt],
                                ALU.mult, ALU.add)
                        last.then_inc(feat_ready, 1)
                    if not last_section:
                        dve.wait_ge(dve_step, steps.next())
                        pt = basis_parts(entry(first, e)[1])
                        if pt:
                            nc.vector.tensor_tensor(a2[0:pt], a[0:pt], a[0:pt], ALU.mult).then_inc(basis_a, 1)
                    q = e - LO_LAG
                    if not (first and q < -EDGE_TILES) and not (last_section and q >= 0):
                        parts = P if entry(first, q)[1] < FEATS else 3 * HALO
                        dve.wait_ge(feat_ready, tile_count(i, q))
                        dve.wait_ge(hi_ready, T_AT[1] + tile_count(i, q))
                        nc.vector.tensor_tensor(tile_part(first, q, 1), FT[q % 3][0:parts],
                                                tile_part(first, q, 0).bitcast(F32), ALU.subtract)\
                            .then_inc(lo_ready, 1)
                    if not first and e == TAIL_AT:
                        tail(i * 2 - 2, 0, 2)
                    if not first and e == UPDATE2_AT:
                        update(2, i * 2 - 1, 1)
                    if not first and e == TAIL2_AT:
                        tail(i * 2 - 1, 1, 2)
                    if e == UPDATE_AT:
                        update(2, i * 2, 0)
                if not first and not last_section:
                    assert steps.n == PAIR_LINKS

            for tile, b in ORDER:
                if tile == "rows":
                    split_rows(3, b)
                else:
                    split_halo(3, b)
                    if b == 0:
                        update(2, B - 1, 1)
                        tail(B - 1, 1, 2)
                    else:
                        update(3, b - 1, (b - 1) % 2)
            update(3, B - 1, 1)

        @block.tensor
        def _(pe):
            pe.wait_ge(const_loaded, 112)

            def group_means(par, n):
                pe.wait_ge(nv_ready, n - 1)
                pe.wait_ge(mv_ready, n)
                nc.tensor.matmul(STAT_BANK[:, 2 * par:2 * par + 2], G[:, :], MV[:, par, :],
                                 start=True, stop=True).then_inc(group_ready, 1)

            def turn_taps(src, pick, co, columns):
                for q in range(columns // co):
                    last = nc.tensor.matmul(TR_BANK[0:KC, q * co:(q + 1) * co], src[:, q, :], pick,
                                            start=True, stop=True)
                last.then_inc(turned, 1)

            def turn_cell(k, h, n):
                pe.wait_ge(taps_ready, at_half(h, NC, n))
                pass_wait(pe, passed["pe"])
                groups = LAYERS[k][1]
                m = len(groups)
                step = (groups[-1] - groups[0]) // (m - 1) if m > 1 else 1
                pick = IDF[:, :].rearrange("o (g c) -> o g c", c=C)[:, groups[0]:groups[-1] + 1:step]
                turn_taps(RAWR, pick, m * C, CELL_COLUMNS[k])

            def halo_taps(n_in, columns, part, g):
                if n_in is None:
                    return WT[:, part, :].rearrange("k (t g n) -> k g t n", t=K3, g=K3)[:, g]
                if n_in == NG:
                    n = columns // NG
                    return WT[:, part, g * n:(g + 1) * n]
                return WT[:, part, 0:columns].rearrange("k (i d o) -> k d i o", i=n_in, d=K3)[:, g]

            def build_banded(n_in, columns, h, at, n_turned, chunks=range(CHUNKS), plain=False):
                if 0 in chunks:
                    pe.wait_ge(turned_hi, n_turned)
                    pe.wait_ge(turned_lo, n_turned)
                for c in chunks:
                    cc = at + c
                    for part, banks, free, built in ((0, BUILD_HI, w_hi, chunk_hi), (1, BUILD_LO, w_lo, chunk_lo)):
                        if cc >= 2:
                            pe.wait_ge(free, at_half(h, CH, cc - 1))
                        bank = banks[cc % 2]
                        if plain and c == TRIPLE:
                            s = TRIPLE * P
                            last = nc.tensor.matmul(bank[0:3 * HALO, 0:columns], SEL[:, s:s + 3 * HALO],
                                                    WT[:, part, 0:columns], start=True, stop=True)
                        elif c < TRIPLE:
                            last = nc.tensor.matmul(bank[:, 0:columns], SEL[:, c * P:(c + 1) * P],
                                                    WT[:, part, 0:columns], start=True, stop=True)
                        else:
                            for g in range(NG):
                                s = TRIPLE * P + g * 3 * HALO
                                last = nc.tensor.matmul(bank[0:3 * HALO, 0:columns // K3], SEL[:, s:s + 3 * HALO],
                                                        halo_taps(n_in, columns, part, g),
                                                        start=g == 0, stop=g == NG - 1)
                        last.then_inc(built, 1)

            ALL_DX = range(K3)
            PRODUCTS = ((0, 0), (0, 1), (1, 0))

            def convolve(bank, parity, terms, open_, close):
                todo = [(tile + i * step, slot, rows, dx, wp, fp) for tile, step, slot, rows, shifts in terms
                        for i, dx in enumerate(shifts) for wp, fp in PRODUCTS]
                for n, (tile, slot, rows, dx, wp, fp) in enumerate(todo):
                    if isinstance(slot, int):
                        moving = F[0:rows, slot, fp]
                    else:
                        moving = slot[:, fp].rearrange("p (y w) -> p y w", w=PW)
                    last = nc.tensor.matmul(bank[:, :].rearrange("p (y x) -> p y x", x=WD),
                                            W[0:rows, parity, wp, tile, :], moving[:, :, dx:dx + WD],
                                            start=open_ and n == 0, stop=close and n == len(todo) - 1)
                return last

            def last_sum(k, j):
                for before in range(k - 1, -1, -1):
                    m = len(cells[before][2])
                    if m > 1 and j < m:
                        return outs_before[before + 1] - m + j + 1
                    if m == 1 and j < 2:
                        return outs_before[before + 1] - 1 + j
                return 0

            def cell_step(h, k, b, par):
                _, ins, outs = cells[k]
                n, m = len(ins), len(outs)
                if b == 0:
                    pe.wait_ge(w_hi, h * CH + chunks_before[k + 1])
                    pe.wait_ge(w_lo, h * CH + chunks_before[k + 1])
                at = b * image_tiles[k] + (tiles_before[k] + image_tiles[k])
                pe.wait_ge(hi_ready, h * TH + at)
                pe.wait_ge(lo_ready, h * TH + at)
                for o in range(m):
                    in_turn = 1 if m > 1 else 2
                    if b >= in_turn:
                        pe.wait_ge(evac_done, h * OH + (outs_before[k] + (b - in_turn) * m + o + 1))
                    elif last_sum(k, o if m > 1 else b):
                        pe.wait_ge(evac_done, h * OH + last_sum(k, o if m > 1 else b))
                    terms = [(g * K3 * m + o, m, par * 4 + g, P, ALL_DX) for g in range(n)]
                    if n == NG:
                        terms.append((MAIN_TILES + o, m, par * 4 + n, 3 * HALO, ALL_DX))
                    else:
                        terms += [(MAIN_TILES + g * m + o, 0, par * 4 + n + g, 3 * HALO, (1,)) for g in range(n)]
                    convolve(out_bank(outs, o, par), k % 2, terms, True, True).then_inc(out_done, 1)

            pe.wait_ge(sel_ready, 1)
            turn_cell(0, None, 1)
            build_banded(LAYERS[0][0], CELL_COLUMNS[0], None, 0, 1)
            pe.wait_ge(bias_rep, 1)
            nc.tensor.matmul(OUT_BANK[0][:, 0:NG * C], BN_REP[:, :, :].rearrange("k y c -> k (y c)"), IDF[:, :],
                             start=True, stop=True)
            nc.tensor.matmul(OUT_BANK[0][:, 64:66], OB_REP[:, :, :].rearrange("k y c -> k (y c)"), IDF[0:2, 0:2],
                             start=True, stop=True).then_inc(bias_done, 1)
            pe.wait_ge(mv_ready, 1)
            nc.tensor.matmul(STAT_BANK[:, 0:2 * B], G[:, :], MV[:, :, :].rearrange("p b a -> p (b a)"),
                             start=True, stop=True).then_inc(group_ready, 1)

            pe.wait_ge(bias_ready, 1)
            with pe.Fori(0, HALVES) as h:
                turn_cell(1, h, 2)
                for k, (_, ins, outs) in enumerate(cells):
                    for b in range(NB):
                        cell_step(h, k, b, b % 2)
                        if k == NC - 1 and b:
                            img = h * NB + (b - 1)
                            group_means((b - 1) % 2, img + 2)
                        build_banded(LAYERS[k + 1][0], CELL_COLUMNS[k + 1], h, chunks_before[k + 1],
                                     h * NC + (k + 2), CHUNKS_AT[b])
                        if b == TURN_AT and k + 2 <= NC:
                            turn_cell(k + 2, h, k + 3)
                img = h * NB + (NB - 1)
                group_means((NB - 1) % 2, img + 2)

            def block_step(blk, b):
                par, slot = b % 2, b % RING * 2
                pe.wait_ge(hi_ready, T_AT[blk - 1] + ORDER_AT["halo", b])
                pe.wait_ge(lo_ready, T_AT[blk - 1] + ORDER_AT["halo", b])
                halo = (MAIN_TILES, 0, slot + 1, 3 * HALO, (1,)) if blk == 1 else \
                    (MAIN_TILES, SINGLE_OUTS, slot + 1, HALO, ALL_DX)
                convolve(OUT_BANK[par], 0, [(0, SINGLE_OUTS, slot, P, ALL_DX), halo], True, True).then_inc(out_done, 1)

            pe.wait_ge(kan_ready, 1)
            turn_taps(KAN, REP, C, KAN_COLUMNS)
            build_banded(None, KAN_COLUMNS, None, C_AT[1], FILL_AT[1] + 1)
            turn_cell(NC, None, HALVES * NC + 2)

            pe.wait_ge(w_hi, C_AT[1])
            pe.wait_ge(w_lo, C_AT[1])
            pe.wait_ge(evac_done, HALVES * OH)
            for b in range(B):
                if b >= 2:
                    pe.wait_ge(added, B + b - 1)
                block_step(1, b)
                if b >= 1:
                    group_means((b - 1) % 2, b - 1 + 2 + B)
            group_means(1, 2 + B + B - 1)

            pe.wait_ge(w_hi, C_AT[2])
            pe.wait_ge(w_lo, C_AT[2])
            pe.wait_ge(added, 2 * B)
            for first, i, tiles in sections(pe, 0):
                for q in tiles:
                    if q < 0:
                        continue
                    par, t = ENTRIES[q]
                    if t == 0 and not first:
                        pe.wait_ge(added, i * 2 + (2 * B + par - 1))
                    pe.wait_ge(hi_ready, T_AT[1] + tile_count(i, q))
                    pe.wait_ge(lo_ready, T_AT[1] + tile_count(i, q))
                    convolve(OUT_BANK[par], 1, [(t * K3, 1, q % RING2, P, ALL_DX)], t == 0, False)\
                        .then_inc(tile_used, 1)
                    if first and q == BUILD_AT:
                        build_banded(1, CELL_COLUMNS[NC], None, C_AT[2], FILL_AT[2] + 1, plain=True)
                    if t == FEATS - 1:
                        for h in range(HALO_FEATS):
                            for k in range(q - t + HALO_FEATS * h, q - t + HALO_FEATS * (h + 1)):
                                pe.wait_ge(halo_rows[k % RING2], i * (PAIR // RING2 * 32) + (k // RING2 + 1) * 32)
                            term = (MAIN_TILES + h * K3, 1, halo_tile(par, h), 3 * HALO, ALL_DX)
                            convolve(OUT_BANK[par], 1, [term], False, h == HALO_FEATS - 1).then_inc(tile_used, 1)
                    if q == 4 and not first:
                        group_means(1, i * 2 + (1 + 2 * B))
                    if q == 13:
                        group_means(0, i * 2 + (2 + 2 * B))

            pe.wait_ge(w_hi, C_AT[2] + CHUNKS)
            pe.wait_ge(w_lo, C_AT[2] + CHUNKS)
            pe.wait_ge(added, 3 * B - 1)
            for b in range(B):
                if b == 1:
                    group_means(1, 1 + 3 * B)
                if b >= 2:
                    pe.wait_ge(out_staged, b - 1)
                block_step(3, b)


_INS = ["x", "L0_conv_W", "L0_conv_b", "L1_conv_weight", "L2_conv_base_weight", "L2_conv_spline_weight",
        "L2_conv_spline_scaler", "L2_conv_bias_weight", "L3_conv_combinator", "L3_conv_bias"]


def shape_constants():
    n_sel = TRIPLE * P + NG * 3 * HALO
    c = np.zeros((P, P + NG * C + CB_COLUMNS + n_sel), np.float32)
    ch = np.arange(P) % C
    c[:, 0:P] = (ch[:, None] // 2 == ch[None, :] // 2) / 16.0
    c[0:NG * C, P:P + NG * C] = np.eye(NG * C)
    at = P + NG * C
    for i in range(BASES):
        c[:, at + i] = 3.5 - i
    for t in range(3):
        c[:, at + BASES + t] = 3.5 - (3 * t + np.arange(P) // HALO)
    for side in range(2):
        c[:, at + BASES + 3 + side] = np.arange(P) // C % 2 == side
    for j in range(YI):
        c[:, at + BASES + 5 + j] = np.abs(np.arange(P) // C - j) <= 1
    for g in range(C // NJ):
        c[:, at + BASES + 5 + YI + g] = np.arange(P) // C == g
    for o in range(C):
        c[:, at + BASES + 5 + 2 * YI + o] = ch == o
    at += CB_COLUMNS
    ky, k_c = np.arange(KC) // C, np.arange(KC) % C
    for j in range(YI):
        s = at + j % TRIPLE * P
        c[0:KC, s:s + P] += (np.arange(P) // C == j + ky[:, None] - 1) & (ch == k_c[:, None])
    rows = np.arange(3 * HALO)
    for g in range(NG):
        s = at + TRIPLE * P + g * 3 * HALO
        c[0:KC, s:s + 3 * HALO] = ((rows // HALO == g) & (ky[:, None] == 2 * (rows // C % 2))
                                   & (rows % C == k_c[:, None]))
    return c


def kernel(**inputs):
    import concourse.bacc as bacc
    from concourse.bass_utils import run_bass_kernel_spmd

    nc = bacc.Bacc("TRN2", target_bir_lowering=False, num_devices=1)
    arrays, args = {}, []
    for name in _INS:
        a = np.ascontiguousarray(inputs[name])
        arrays[f"in_{name}"] = a
        args.append(nc.dram_tensor(f"in_{name}", a.shape, mybir.dt.from_np(a.dtype), kind="ExternalInput").ap())
    consts = shape_constants()
    arrays["in_consts"] = consts
    args.append(nc.dram_tensor("in_consts", consts.shape, mybir.dt.float32, kind="ExternalInput").ap())
    out = nc.dram_tensor("out_0", (B, C, YI * YB, WD), mybir.dt.float32, kind="ExternalOutput").ap()
    build(nc, *args, out)
    r = run_bass_kernel_spmd(nc, [arrays], core_ids=[0])
    return r.results[0]["out_0"]
```
